# Optimizing a Trainium2 kernel written in Bass

```python
import numpy as np
import jax
import jax.numpy as jnp

def _softmax(x, axis=-1):
    return jax.nn.softmax(x, axis=axis)

def _gelu(x):
    return jax.nn.gelu(x, approximate=True)

def _silu(x):
    return jax.nn.silu(x)

def _sigmoid(x):
    return jax.nn.sigmoid(x)

def _layernorm(x, axis=-1, eps=1e-05):
    m = jnp.mean(x, axis=axis, keepdims=True)
    v = jnp.var(x, axis=axis, keepdims=True)
    return (x - m) / jnp.sqrt(v + eps)

def _scatter_add(tgt, idx, src, axis=0):
    return tgt.at[idx].add(src)

def _segment_sum(src, seg, n):
    return jax.ops.segment_sum(src, seg, n)
kernel_name = 'mk_xattn_seq_d2_seqx_r4_a4f9e6'

def setup_inputs(seed: int=0):
    np.random.seed(seed)
    _w = jnp.asarray

    def _rec_inputs():
        import jax
        import jax.numpy as jnp
        _rk = jax.random.key(seed)
        x = -0.0002928 + 1 * jax.random.normal(jax.random.fold_in(_rk, 1), (2, 1024, 256), jnp.float32)
        _lenS = 1024 - jax.random.randint(jax.random.fold_in(_rk, 7), (2,), 0, max(1, 1024 // 4) + 1, jnp.int32)
        _lenS2 = 77 - jax.random.randint(jax.random.fold_in(_rk, 8), (2,), 0, max(1, 77 // 4) + 1, jnp.int32)
        _ctx_1024P = jax.random.normal(jax.random.fold_in(_rk, 11), (2, 16, 256), jnp.float32)
        _ctx_1024c = jax.random.dirichlet(jax.random.fold_in(_rk, 511), 0.3 * jnp.ones((16,), jnp.float32), (2, 77))
        _ctx_1024t = jnp.einsum('bsk,bkd->bsd', _ctx_1024c, _ctx_1024P)
        _ctx_1024t = _ctx_1024t * jax.lax.rsqrt(jnp.mean(jnp.square(_ctx_1024t)) + 1e-12) * 0.953939
        ctx_1024 = -1.39393e-06 + 0.999914 * (_ctx_1024t + 0.3 * jax.random.normal(jax.random.fold_in(_rk, 611), (2, 77, 256), jnp.float32))
        return (x, ctx_1024)
    x, ctx_1024 = _rec_inputs()

    def _L0_xattn_setup():
        import jax, jax.numpy as jnp
        import numpy as np
        B, S, D, H = (2, 512, 256, 16)
        DH = D // H

        def _split_heads(x):
            bsz, slen, _ = x.shape
            return x.reshape(bsz, slen, H, DH).transpose(2, 0, 1, 3)
        key = jax.random.key(seed)
        ks = jax.random.split(key, 9)

        def rn(k, shape, scale=1.0):
            return jax.random.normal(k, shape, dtype=jnp.float32) * scale
        w_scale = 1.0 / np.sqrt(D)
        return {'queries': rn(ks[0], (B, S, D)), 'keys': rn(ks[1], (B, S, D)), 'values': rn(ks[2], (B, S, D)), 'Wq': rn(ks[3], (D, D), w_scale), 'bq': rn(ks[4], (D,), w_scale), 'Wk': rn(ks[5], (D, D), w_scale), 'bk': rn(ks[6], (D,), w_scale), 'Wv': rn(ks[7], (D, D), w_scale), 'bv': rn(ks[8], (D,), w_scale)}
    _L0_xattn_all = _L0_xattn_setup()
    _L0_xattn_in = {k: v for k, v in _L0_xattn_all.items() if k in ('Wq', 'bq', 'Wk', 'bk', 'Wv', 'bv')}
    del _L0_xattn_all

    def _L1_xattn_setup():
        import jax, jax.numpy as jnp
        import numpy as np
        D = 256
        H = 16
        HD = D // H
        DFF = 1024
        B, Q, S = (4, 64, 2048)
        EPS = 1e-05

        def layernorm(x, g, b):
            mu = jnp.mean(x, axis=-1, keepdims=True)
            var = jnp.mean(jnp.square(x - mu), axis=-1, keepdims=True)
            return (x - mu) * jax.lax.rsqrt(var + EPS) * g + b

        def split_heads(x):
            b, t, _ = x.shape
            return x.reshape(b, t, H, HD).transpose(0, 2, 1, 3)

        def merge_heads(x):
            b, h, t, hd = x.shape
            return x.transpose(0, 2, 1, 3).reshape(b, t, h * hd)

        def attention(q, k, v):
            scale = 1.0 / jnp.sqrt(jnp.asarray(HD, q.dtype))
            scores = jnp.einsum('bhqd,bhkd->bhqk', q, k) * scale
            attn = jax.nn.softmax(scores, axis=-1)
            return jnp.einsum('bhqk,bhkd->bhqd', attn, v)
        key = jax.random.key(seed)
        ks = jax.random.split(key, 12)
        s = 0.02
        rn = lambda k, shp: jax.random.normal(k, shp, dtype=jnp.float32) * s
        return {'queries': jax.random.normal(ks[0], (B, Q, D), dtype=jnp.float32), 'context': jax.random.normal(ks[1], (B, S, D), dtype=jnp.float32), 'sa_in_w': rn(ks[2], (3 * D, D)), 'sa_in_b': jnp.zeros((3 * D,), jnp.float32), 'sa_out_w': rn(ks[3], (D, D)), 'sa_out_b': jnp.zeros((D,), jnp.float32), 'ln1_g': jnp.ones((D,), jnp.float32), 'ln1_b': jnp.zeros((D,), jnp.float32), 'cq_w': rn(ks[4], (D, D)), 'cq_b': jnp.zeros((D,), jnp.float32), 'ck_w': rn(ks[5], (D, D)), 'ck_b': jnp.zeros((D,), jnp.float32), 'cv_w': rn(ks[6], (D, D)), 'cv_b': jnp.zeros((D,), jnp.float32), 'co_w': rn(ks[7], (D, D)), 'co_b': jnp.zeros((D,), jnp.float32), 'ln2_g': jnp.ones((D,), jnp.float32), 'ln2_b': jnp.zeros((D,), jnp.float32), 'w1': rn(ks[8], (DFF, D)), 'b1': jnp.zeros((DFF,), jnp.float32), 'w2': rn(ks[9], (D, DFF)), 'b2': jnp.zeros((D,), jnp.float32), 'ln3_g': jnp.ones((D,), jnp.float32), 'ln3_b': jnp.zeros((D,), jnp.float32)}
    _L1_xattn_all = _L1_xattn_setup()
    _L1_xattn_in = {k: v for k, v in _L1_xattn_all.items() if k in ('sa_in_w', 'sa_in_b', 'sa_out_w', 'sa_out_b', 'ln1_g', 'ln1_b', 'cq_w', 'cq_b', 'ck_w', 'ck_b', 'cv_w', 'cv_b', 'co_w', 'co_b', 'ln2_g', 'ln2_b', 'w1', 'b1', 'w2', 'b2', 'ln3_g', 'ln3_b')}
    del _L1_xattn_all
    return {'x': x, 'ctx_1024': ctx_1024, 'L0_xattn_Wq': _L0_xattn_in['Wq'], 'L0_xattn_bq': _L0_xattn_in['bq'], 'L0_xattn_Wk': _L0_xattn_in['Wk'], 'L0_xattn_bk': _L0_xattn_in['bk'], 'L0_xattn_Wv': _L0_xattn_in['Wv'], 'L0_xattn_bv': _L0_xattn_in['bv'], 'L1_xattn_sa_in_w': _L1_xattn_in['sa_in_w'], 'L1_xattn_sa_in_b': _L1_xattn_in['sa_in_b'], 'L1_xattn_sa_out_w': _L1_xattn_in['sa_out_w'], 'L1_xattn_sa_out_b': _L1_xattn_in['sa_out_b'], 'L1_xattn_ln1_g': _L1_xattn_in['ln1_g'], 'L1_xattn_ln1_b': _L1_xattn_in['ln1_b'], 'L1_xattn_cq_w': _L1_xattn_in['cq_w'], 'L1_xattn_cq_b': _L1_xattn_in['cq_b'], 'L1_xattn_ck_w': _L1_xattn_in['ck_w'], 'L1_xattn_ck_b': _L1_xattn_in['ck_b'], 'L1_xattn_cv_w': _L1_xattn_in['cv_w'], 'L1_xattn_cv_b': _L1_xattn_in['cv_b'], 'L1_xattn_co_w': _L1_xattn_in['co_w'], 'L1_xattn_co_b': _L1_xattn_in['co_b'], 'L1_xattn_ln2_g': _L1_xattn_in['ln2_g'], 'L1_xattn_ln2_b': _L1_xattn_in['ln2_b'], 'L1_xattn_w1': _L1_xattn_in['w1'], 'L1_xattn_b1': _L1_xattn_in['b1'], 'L1_xattn_w2': _L1_xattn_in['w2'], 'L1_xattn_b2': _L1_xattn_in['b2'], 'L1_xattn_ln3_g': _L1_xattn_in['ln3_g'], 'L1_xattn_ln3_b': _L1_xattn_in['ln3_b']}

def reference(x, ctx_1024, L0_xattn_Wq, L0_xattn_bq, L0_xattn_Wk, L0_xattn_bk, L0_xattn_Wv, L0_xattn_bv, L1_xattn_sa_in_w, L1_xattn_sa_in_b, L1_xattn_sa_out_w, L1_xattn_sa_out_b, L1_xattn_ln1_g, L1_xattn_ln1_b, L1_xattn_cq_w, L1_xattn_cq_b, L1_xattn_ck_w, L1_xattn_ck_b, L1_xattn_cv_w, L1_xattn_cv_b, L1_xattn_co_w, L1_xattn_co_b, L1_xattn_ln2_g, L1_xattn_ln2_b, L1_xattn_w1, L1_xattn_b1, L1_xattn_w2, L1_xattn_b2, L1_xattn_ln3_g, L1_xattn_ln3_b):
    import jax
    import jax.numpy as jnp

    def _L0_xattn_ref(queries, keys, values, Wq, bq, Wk, bk, Wv, bv):
        import jax, jax.numpy as jnp
        import numpy as np
        B, S, D, H = (2, 512, 256, 16)
        DH = D // H

        def _split_heads(x):
            bsz, slen, _ = x.shape
            return x.reshape(bsz, slen, H, DH).transpose(2, 0, 1, 3)
        Q = queries @ Wq + bq
        K = keys @ Wk + bk
        V = values @ Wv + bv
        Qh = _split_heads(Q)
        Kh = _split_heads(K)
        Vh = _split_heads(V)
        scale = 1.0 / jnp.sqrt(jnp.asarray(DH, dtype=Qh.dtype))
        scores = jnp.einsum('hbqd,hbkd->hbqk', Qh, Kh) * scale
        attn = jax.nn.softmax(scores, axis=-1)
        out = jnp.einsum('hbqk,hbkd->hbqd', attn, Vh)
        out = out.transpose(1, 2, 0, 3).reshape(queries.shape[0], queries.shape[1], D)
        return out + queries

    def _L1_xattn_ref(queries, context, sa_in_w, sa_in_b, sa_out_w, sa_out_b, ln1_g, ln1_b, cq_w, cq_b, ck_w, ck_b, cv_w, cv_b, co_w, co_b, ln2_g, ln2_b, w1, b1, w2, b2, ln3_g, ln3_b):
        import jax, jax.numpy as jnp
        import numpy as np
        D = 256
        H = 16
        HD = D // H
        DFF = 1024
        B, Q, S = (4, 64, 2048)
        EPS = 1e-05

        def layernorm(x, g, b):
            mu = jnp.mean(x, axis=-1, keepdims=True)
            var = jnp.mean(jnp.square(x - mu), axis=-1, keepdims=True)
            return (x - mu) * jax.lax.rsqrt(var + EPS) * g + b

        def split_heads(x):
            b, t, _ = x.shape
            return x.reshape(b, t, H, HD).transpose(0, 2, 1, 3)

        def merge_heads(x):
            b, h, t, hd = x.shape
            return x.transpose(0, 2, 1, 3).reshape(b, t, h * hd)

        def attention(q, k, v):
            scale = 1.0 / jnp.sqrt(jnp.asarray(HD, q.dtype))
            scores = jnp.einsum('bhqd,bhkd->bhqk', q, k) * scale
            attn = jax.nn.softmax(scores, axis=-1)
            return jnp.einsum('bhqk,bhkd->bhqd', attn, v)
        qn = layernorm(queries, ln1_g, ln1_b)
        qkv = qn @ sa_in_w.T + sa_in_b
        q, k, v = jnp.split(qkv, 3, axis=-1)
        sa = merge_heads(attention(split_heads(q), split_heads(k), split_heads(v)))
        sa = sa @ sa_out_w.T + sa_out_b
        x = queries + sa
        xn = layernorm(x, ln2_g, ln2_b)
        cq = split_heads(xn @ cq_w.T + cq_b)
        ck = split_heads(context @ ck_w.T + ck_b)
        cv = split_heads(context @ cv_w.T + cv_b)
        ca = merge_heads(attention(cq, ck, cv))
        ca = ca @ co_w.T + co_b
        x = x + ca
        xn = layernorm(x, ln3_g, ln3_b)
        h = jax.nn.gelu(xn @ w1.T + b1, approximate=False)
        x = x + (h @ w2.T + b2)
        return x
    x = _L0_xattn_ref(x, ctx_1024, ctx_1024, L0_xattn_Wq, L0_xattn_bq, L0_xattn_Wk, L0_xattn_bk, L0_xattn_Wv, L0_xattn_bv)
    x = _L1_xattn_ref(x, ctx_1024, L1_xattn_sa_in_w, L1_xattn_sa_in_b, L1_xattn_sa_out_w, L1_xattn_sa_out_b, L1_xattn_ln1_g, L1_xattn_ln1_b, L1_xattn_cq_w, L1_xattn_cq_b, L1_xattn_ck_w, L1_xattn_ck_b, L1_xattn_cv_w, L1_xattn_cv_b, L1_xattn_co_w, L1_xattn_co_b, L1_xattn_ln2_g, L1_xattn_ln2_b, L1_xattn_w1, L1_xattn_b1, L1_xattn_w2, L1_xattn_b2, L1_xattn_ln3_g, L1_xattn_ln3_b)
    return x

_drawn_inputs = setup_inputs


def setup_inputs(seed=0):
    import zlib

    import numpy as np

    out = dict(_drawn_inputs(seed))
    spreads = {'L1_xattn_sa_in_b': (0.0, 0.28),
     'L1_xattn_sa_out_b': (0.0, 0.1),
     'L1_xattn_ln1_g': (1.0, 0.6),
     'L1_xattn_ln1_b': (0.0, 0.8),
     'L1_xattn_cq_b': (0.0, 0.8),
     'L1_xattn_ck_b': (0.0, 0.8),
     'L1_xattn_cv_b': (0.0, 0.292),
     'L1_xattn_co_b': (0.0, 0.1),
     'L1_xattn_ln2_g': (1.0, 0.6),
     'L1_xattn_ln2_b': (0.0, 0.8),
     'L1_xattn_b1': (0.0, 0.281),
     'L1_xattn_b2': (0.0, 0.1),
     'L1_xattn_ln3_g': (1.0, 0.6),
     'L1_xattn_ln3_b': (0.0, 0.8)}
    factors = {'L0_xattn_bq': 4.17, 'L0_xattn_bk': 8.0, 'L1_xattn_cq_w': 8.0, 'L1_xattn_ck_w': 8.0}
    for name, (base, spread) in spreads.items():
        noise = np.random.default_rng([zlib.crc32(name.encode()), seed]).standard_normal(out[name].shape)
        drawn = base * np.exp(spread * noise) if base else spread * noise
        out[name] = jnp.asarray(drawn.astype(out[name].dtype))
    for name, factor in factors.items():
        out[name] = (out[name] * factor).astype(out[name].dtype)
    return out
```

```python
import concourse.bass as bass
from concourse import mybir
from contextlib import ExitStack

FP32 = mybir.dt.float32
BF16 = mybir.dt.bfloat16
ALU = mybir.AluOpType
ACT = mybir.ActivationFunctionType
AX = mybir.AxisListType

BATCH, SEQ, DIM = 2, 1024, 256
HEADS = 16
HD = DIM // HEADS
CTX = 77
TOK = BATCH * SEQ
FF = 1024
EPS = 1e-5
SCALE = HD ** -0.5

P = 128
KC = DIM // P
NT = TOK // P
BLK = 512
NB = TOK // BLK
TPB = BLK // P
QUAD = 4
NG = BATCH * HEADS // QUAD
HALVES = SEQ // BLK
NQ = NG * HALVES
PARTS = 3
BANDS = [(0, 0), (0, 1), (0, 2), (1, 0), (1, 1), (2, 0)]
SROWS = len(BANDS) * HD
MROWS = SROWS + PARTS
NBUF = 3


class Attention:

    def __init__(self, name, key_tiles, keys):
        self.name = name
        self.kt = key_tiles
        self.keys = keys
        self.steps = NQ * key_tiles
        self.whole = key_tiles > 1
        self.units = TPB * (QUAD if self.whole else 1)
        self.upb = self.units // key_tiles
        self.mt_at = 1 if self.whole else 0


SELF = Attention("self", SEQ // P, P)
CROSS = Attention("cross", 1, CTX)


def xattn_kernel(nc, xT_d, x_d, cT_d, ident_d, wq0, bq0, wk0, bk0, wv0, bv0,
                 sa_w, sa_b, so_w, so_b, g1, b1n, cqw, cqb, ckw, ckb, cvw, cvb, cow, cob,
                 g2, b2n, w1, b1, w2, b2, g3, b3n, out):
    q_parts = nc.dram_tensor("q_parts", [3, PARTS, DIM, TOK], BF16).ap()
    k_parts = nc.dram_tensor("k_parts", [PARTS, DIM, TOK], BF16).ap()
    c_parts = nc.dram_tensor("c_parts", [2, PARTS, DIM, BATCH * CTX], BF16).ap()

    ctx = ExitStack()
    with ctx:
        def sb(name, shape, dt=FP32):
            return ctx.enter_context(nc.sbuf_tensor(name, shape, dt))

        def sem(name):
            return ctx.enter_context(nc.semaphore(name))

        fm = sb("fm", [P, KC, TOK])
        X = sb("X", [P, NT, DIM])
        A = sb("A", [P, NT, DIM])
        V = sb("V", [P, NT, DIM])
        w_q0 = sb("w_q0", [P, KC, DIM]); w_k0 = sb("w_k0", [P, KC, DIM]); w_v0 = sb("w_v0", [P, KC, DIM])
        w_sa = sb("w_sa", [P, KC, 3 * DIM]); w_so = sb("w_so", [P, KC, DIM])
        w_cq = sb("w_cq", [P, KC, DIM]); w_ck = sb("w_ck", [P, KC, DIM])
        w_cv = sb("w_cv", [P, KC, DIM]); w_co = sb("w_co", [P, KC, DIM])
        w_1 = V[:, 0:8, :].rearrange("p a b -> p (a b)").rearrange("p (k f) -> p k f", k=KC)
        w_2 = V[:, 8:16, :]
        ctxT = sb("ctxT", [P, KC, BATCH * CTX])
        Vc = sb("Vc", [P, 2, BATCH, DIM])
        stacks = sb("stacks", [P, NBUF, 2, QUAD, SEQ], BF16)
        Kst = [stacks[:, n, 0] for n in range(NBUF)]
        Qst = [stacks[:, n, 1] for n in range(NBUF)]
        Vst = sb("Vst", [P, 2, SELF.kt, QUAD, 32])
        prob = sb("prob", [P, 2, QUAD, BLK])
        hid = sb("hid", [P, FF // P, BLK])
        pvT = sb("pvT", [P, 2, BLK])
        q32 = sb("q32", [P, 2, BLK]); r32 = sb("r32", [P, 2, BLK])
        split = sb("split", [P, 2, PARTS, BLK], BF16)
        mrow = sb("mrow", [PARTS * QUAD, 2, BLK], BF16)
        nm = sb("nm", [P, 2, TPB, QUAD])
        nr = sb("nr", [P, 2, TPB, QUAD])
        mp = sb("mp", [P, 2, TPB, PARTS, QUAD], BF16)
        rden = sb("rden", [P, 2, TPB, QUAD])
        ident = sb("ident", [P, P])
        identb = sb("identb", [P, P], BF16)
        cols = sb("cols", [P, 40])
        bc = sb("bc", [P, 6, DIM])
        stats = sb("stats", [P, NT, 6])
        mv = sb("mv", [P, NT, 2])
        rstd = sb("rstd", [P, NT])
        nexp = sb("nexp", [P, NT])

        SM = ctx.enter_context(nc.psum_tensor("SM", [P, 2, 2 * BLK], FP32))
        ST = ctx.enter_context(nc.psum_tensor("ST", [P, 2, BLK], FP32))
        PV = ctx.enter_context(nc.psum_tensor("PV", [P, BLK], FP32))
        MI = ctx.enter_context(nc.psum_tensor("MI", [P, BLK], FP32))
        MIb = MI[:, :].bitcast(BF16)
        ring = [SM[:, 0, 0:BLK], SM[:, 0, BLK:], SM[:, 1, 0:BLK], SM[:, 1, BLK:]]

        C_BQ0, C_BK0, C_SAQ, C_SAK, C_CQ, C_CK = 0, 2, 4, 6, 8, 10
        C_G1, C_B1, C_G2, C_B2, C_G3, C_B3, C_F1 = 12, 14, 16, 18, 20, 22, 24
        B_V0, B_VS, B_SO, B_CV, B_CO, B_F2 = range(6)

        in_first = sem("in_first"); in_x = sem("in_x"); in_w = sem("in_w"); in_b = sem("in_b")
        in_ffn = sem("in_ffn")
        const_ready = sem("const_ready")
        ident_ready = sem("ident_ready")
        bias_scaled = sem("bias_scaled")
        out_done = sem("out_done")
        in_counts = {}

        mm_ready = sem("mm_ready")
        q32_ready = sem("q32_ready"); part1_ready = sem("part1_ready"); rest1_ready = sem("rest1_ready")
        part2_ready = sem("part2_ready"); parts_ready = sem("parts_ready")
        parts_stored = [sem("parts_stored0"), sem("parts_stored1")]
        fm_ready = sem("fm_ready")
        stat_ready = sem("stat_ready"); mv_ready = sem("mv_ready"); rstd_ready = sem("rstd_ready")
        norm_ready = sem("norm_ready")
        x_ready = sem("x_ready")
        v_ready = sem("v_ready")
        bias_added = sem("bias_added")
        hid_ready = sem("hid_ready")
        var_ready = sem("var_ready")

        BPR = len(ring)

        ring_at, total = {}, 0
        for name, count in [("proj_q0", 8), ("proj_k0", 2), ("proj_kc", 2), ("vals_c", 4),
                            ("t_ln1", 8), ("proj_q1", 8), ("proj_k1", 8), ("vals_s", 16),
                            ("t_a1", 8), ("out_1", 16), ("t_ln2", 8), ("proj_q2", 8),
                            ("t_a2", 8), ("out_2", 16), ("t_ln3", 8), ("ffn", 48)]:
            ring_at[name] = total
            total += count
        def read_out(n):
            stage = [k for k in ring_at if ring_at[k] <= n][-1]
            i = n - ring_at[stage]
            if stage in split_at:
                return q32_ready, split_at[stage] + i + 1
            if stage == "ffn":
                tb, f = divmod(i, FF // P + TPB)
                return (hid_ready, tb * (FF // P) + f + 1) if f < FF // P else \
                    (x_ready, 3 * NT + tb * TPB + f - FF // P + 1)
            who, before = {"vals_c": (v_ready, 0), "vals_s": (v_ready, 4), "out_1": (x_ready, NT),
                           "out_2": (x_ready, 2 * NT), "t_ln1": (fm_ready, 0), "t_a1": (fm_ready, 8),
                           "t_ln2": (fm_ready, 16), "t_a2": (fm_ready, 24), "t_ln3": (fm_ready, 32)}[stage]
            return who, before + i + 1

        SPLITS = [
            ("proj_q0", w_q0, 0, C_BQ0, SCALE, "x", q_parts[0]),
            ("proj_k0", w_k0, 0, C_BK0, 1.0, "c", c_parts[0]),
            ("proj_kc", w_ck, 0, C_CK, 1.0, "c", c_parts[1]),
            ("proj_q1", w_sa, 0, C_SAQ, SCALE, "x", q_parts[1]),
            ("proj_k1", w_sa, DIM, C_SAK, 1.0, "x", k_parts),
            ("proj_q2", w_cq, 0, C_CQ, SCALE, "x", q_parts[2]),
        ]
        split_at, total = {}, 0
        for name, *_rest in SPLITS:
            split_at[name] = total
            total += 8 if _rest[4] == "x" else 2

        def split_chunks(name):
            spec = [s for s in SPLITS if s[0] == name][0]
            n = 0
            for tb in range(NB if spec[5] == "x" else 1):
                for mc in range(KC):
                    width = BLK if spec[5] == "x" else BATCH * CTX
                    yield spec, split_at[name] + n, ring_at[name] + n, mc, tb * BLK, width
                    n += 1

        ATT = {}
        for name in ("a0", "a1", "a2"):
            s = ATT[name] = {}
            for what in ("sm_done", "max_done", "mp_ready", "mp_p1", "mp_r1", "mp_p2", "mt_done",
                         "mrow_ready", "st_done", "exp_done", "pv_done", "pv_out", "ot_done",
                         "rd_done", "head_out", "vst_ready"):
                s[what] = sem(f"{name}_{what}")
            s["stack_in"] = [sem(f"{name}_stack{n}") for n in range(NBUF)]
            s["rows_in"] = [sem(f"{name}_rows{n}") for n in range(2)]
        SPEC = {"a0": (CROSS, q_parts[0], c_parts[0], Vc[:, 0]),
                "a1": (SELF, q_parts[1], k_parts, None),
                "a2": (CROSS, q_parts[2], c_parts[1], Vc[:, 1])}
        NSD = 2 * len(BANDS)

        def stored(eng, name):
            last = split_at[name] + (8 if name in ("proj_q0", "proj_q1", "proj_k1", "proj_q2") else 2)
            eng.wait_ge(parts_stored[0], 16 * ((last + 1) // 2))
            eng.wait_ge(parts_stored[1], 16 * (last // 2))

        block = ctx.enter_context(nc.Block())

        @block.sync
        def _(sp):
            sp.dma_start(fm[:, :, :], xT_d.rearrange("(k p) t -> p k t", p=P)).then_inc(in_first, 16)
            sp.dma_start(w_q0[:, :, :], wq0.rearrange("(k p) n -> p k n", p=P)).then_inc(in_first, 16)
            sp.dma_start(ctxT[:, :, :], cT_d.rearrange("(k p) t -> p k t", p=P)).then_inc(in_first, 16)
            sp.dma_start(w_k0[:, :, :], wk0.rearrange("(k p) n -> p k n", p=P)).then_inc(in_first, 16)
            sp.dma_start(ident[:, :], ident_d).then_inc(in_first, 16)
            for tile, src in ((w_v0, wv0), (w_ck, ckw), (w_cv, cvw), (w_sa, sa_w), (w_so, so_w),
                              (w_cq, cqw), (w_co, cow)):
                sp.dma_start(tile[:, :, :], src.rearrange("(k p) n -> p k n", p=P)).then_inc(in_w, 16)
            sp.dma_start(X[:, :, :], x_d.rearrange("(t p) d -> p t d", p=P)).then_inc(in_x, 16)

            def store_parts(name):
                for spec, n, _r, mc, c0, width in split_chunks(name):
                    sp.wait_ge(parts_ready, n + 1)
                    sp.dma_start(spec[6][:, mc * P:(mc + 1) * P, c0:c0 + width].rearrange("r p t -> p r t"),
                                 split[:, n % 2, :, 0:width]).then_inc(parts_stored[n % 2], 16)

            def attention_loads(name, q_name, k_name):
                att, qp, kp, _v = SPEC[name]
                s = ATT[name]
                stored(sp, q_name)
                stored(sp, k_name)

                def stack(g):
                    b, h0 = g // QUAD, (g % QUAD) * QUAD
                    keys = att.kt * att.keys
                    if g >= NBUF:
                        sp.wait_ge(s["st_done"], (g - NBUF + 1) * HALVES * att.kt * QUAD)
                    for band, (kpart, qpart) in enumerate(BANDS):
                        rows = slice(band * HD, (band + 1) * HD)
                        sp.dma_start(Kst[g % NBUF][rows, :, 0:keys],
                                     kp[kpart, h0 * HD:(h0 + QUAD) * HD, b * keys:(b + 1) * keys]
                                     .rearrange("(h d) t -> d h t", d=HD)).then_inc(s["stack_in"][g % NBUF], 16)
                        sp.dma_start(Qst[g % NBUF][rows, :, :],
                                     qp[qpart, h0 * HD:(h0 + QUAD) * HD, b * SEQ:(b + 1) * SEQ]
                                     .rearrange("(h d) t -> d h t", d=HD)).then_inc(s["stack_in"][g % NBUF], 16)

                def rows(q):
                    g, j = q // HALVES, q % HALVES
                    sp.wait_ge(s["mrow_ready"], q + 1)
                    for part in range(PARTS):
                        sp.dma_start(Qst[g % NBUF][SROWS + part:SROWS + part + 1, :, j * BLK:(j + 1) * BLK],
                                     mrow[part * QUAD:(part + 1) * QUAD, q % 2, :]) \
                          .then_inc(s["rows_in"][q % 2], 16)

                for g in range(NBUF):
                    stack(g)
                rows(0)
                for q in range(NQ - 1):
                    if q >= 2 and q % 2 == 0 and q // 2 + 2 < NG:
                        stack(q // 2 + 2)
                    rows(q + 1)

            store_parts("proj_q0")
            store_parts("proj_k0")
            store_parts("proj_kc")
            attention_loads("a0", "proj_q0", "proj_k0")
            store_parts("proj_q1")
            store_parts("proj_k1")
            attention_loads("a1", "proj_q1", "proj_k1")
            sp.wait_ge(ATT["a1"]["vst_ready"], NG)
            sp.dma_start(w_1, w1.rearrange("(k p) n -> p k n", p=P)).then_inc(in_ffn, 16)
            sp.dma_start(w_2, w2.rearrange("(k p) n -> p k n", p=P)).then_inc(in_ffn, 16)
            store_parts("proj_q2")
            attention_loads("a2", "proj_q2", "proj_kc")
            for t in range(NT):
                sp.wait_ge(x_ready, 3 * NT + t + 1)
                sp.dma_start(out[t * P:(t + 1) * P, :], X[:, t, :]).then_inc(out_done, 16)
            sp.wait_ge(out_done, 16 * NT)

        @block.tensor
        def _(pe):
            mm = nc.tensor.matmul

            def bank(n):
                if n >= BPR:
                    pe.wait_ge(*read_out(n - BPR))
                return ring[n % BPR]

            def ring_empty(stage):
                for n in range(ring_at[stage] - BPR, ring_at[stage]):
                    pe.wait_ge(*read_out(n))

            def project(name):
                for spec, _n, r, mc, c0, width in split_chunks(name):
                    _nm, w, w0, *_s, source, _st = spec
                    src = fm if source == "x" else ctxT
                    ps = bank(r)
                    for k in range(KC):
                        last = mm(ps[:, 0:width], w[:, k, w0 + mc * P:w0 + (mc + 1) * P],
                                  src[:, k, c0:c0 + width], start=(k == 0), stop=(k == KC - 1))
                    last.then_inc(mm_ready, 1)

            def context_values():
                r = ring_at["vals_c"]
                for a, w in enumerate((w_v0, w_cv)):
                    for b in range(BATCH):
                        ps = bank(r)
                        for k in range(KC):
                            last = mm(ps[0:CTX, 0:DIM], ctxT[:, k, b * CTX:(b + 1) * CTX], w[:, k, :],
                                      start=(k == 0), stop=(k == KC - 1))
                        last.then_inc(mm_ready, 1)
                        r += 1

            def to_channels(name, ready, ready_at, per_tile):
                r = ring_at[name]
                for tb in range(NB):
                    pe.wait_ge(ready, ready_at + per_tile * (tb + 1))
                    for c in range(KC):
                        ps = bank(r)
                        for i in range(TPB):
                            last = nc.tensor.transpose(ps[:, i * P:(i + 1) * P],
                                                       A[:, tb * TPB + i, c * P:(c + 1) * P], ident[:, :])
                        last.then_inc(mm_ready, 1)
                        r += 1

            def by_token(name, w, w0):
                for t in range(NT):
                    ps = bank(ring_at[name] + t)
                    for k in range(KC):
                        last = mm(ps[:, 0:DIM], fm[:, k, t * P:(t + 1) * P], w[:, k, w0:w0 + DIM],
                                  start=(k == 0), stop=(k == KC - 1))
                    last.then_inc(mm_ready, 1)

            def attention(name):
                att, *_r = SPEC[name]
                s = ATT[name]

                def unit(u):
                    q, v = u // att.units, u % att.units
                    g, j = q // HALVES, q % HALVES
                    if v == 0:
                        if j == 0:
                            pe.wait_ge(s["stack_in"][g % NBUF], 16 * NSD * (g // NBUF + 1))
                    if u >= 2:
                        pe.wait_ge(s["max_done"], u - 1)
                    qt = v // QUAD if att.whole else v
                    c0 = j * BLK + qt * P
                    if att.whole:
                        h = v % QUAD
                        for c in range(2):
                            last = mm(SM[:, u % 2, c * BLK:(c + 1) * BLK], Qst[g % NBUF][0:SROWS, h, c0:c0 + P],
                                      Kst[g % NBUF][0:SROWS, h, c * BLK:(c + 1) * BLK], start=True, stop=True)
                    else:
                        for h in range(QUAD):
                            last = mm(SM[:, u % 2, h * att.keys:(h + 1) * att.keys],
                                      Qst[g % NBUF][0:SROWS, h, c0:c0 + P],
                                      Kst[g % NBUF][0:SROWS, h, 0:att.keys], start=True, stop=True)
                    last.then_inc(s["sm_done"], 1)

                def maxima_to_rows(q):
                    pe.wait_ge(s["mp_ready"], q + 1)
                    if q >= 2:
                        done = sum(1 for x in range(NQ) if out_step(x) < (q - 1) * att.kt + att.mt_at)
                        if done:
                            pe.wait_ge(s["head_out"], done)
                    if q >= 1:
                        pe.wait_ge(s["mrow_ready"], q)
                    for i in range(TPB):
                        last = nc.tensor.transpose(MIb[0:PARTS * QUAD, i * P:(i + 1) * P],
                                                   mp[:, q % 2, i].rearrange("p r h -> p (r h)"), identb[:, :])
                    last.then_inc(s["mt_done"], 1)

                def out_step(q):
                    return (q + 1) * att.kt - 1 + 2

                def scores(t, h):
                    q, kt = t // att.kt, t % att.kt
                    g, j = q // HALVES, q % HALVES
                    n = t * QUAD + h
                    if kt == 0 and h == 0:
                        pe.wait_ge(s["rows_in"][q % 2], 16 * PARTS * (q // 2 + 1))
                    if n >= 2:
                        pe.wait_ge(s["exp_done"], n - 1)
                    mm(ST[0:att.keys, n % 2, :], Kst[g % NBUF][0:MROWS, h, kt * att.keys:(kt + 1) * att.keys],
                       Qst[g % NBUF][0:MROWS, h, j * BLK:(j + 1) * BLK], start=True, stop=True) \
                        .then_inc(s["st_done"], 1)

                def values(t):
                    q, kt = t // att.kt, t % att.kt
                    g = q // HALVES
                    if kt == 0:
                        pe.wait_ge(s["vst_ready"], g + 1)
                        if q >= 1:
                            pe.wait_ge(s["pv_out"], q)
                    pe.wait_ge(s["exp_done"], (t + 1) * QUAD)
                    for h in range(QUAD):
                        last = mm(PV[h * 32:(h + 1) * 32, :], Vst[0:att.keys, g % 2, kt, h, :],
                                  prob[0:att.keys, t % 2, h, :], start=(kt == 0), stop=(kt == att.kt - 1))
                    last.then_inc(s["pv_done"], 1)

                def output_transposes(q):
                    pe.wait_ge(s["pv_out"], q + 1)
                    if q >= 1:
                        pe.wait_ge(s["head_out"], q)
                    rows = sum(1 for x in range(1, NQ) if (x - 1) * att.kt + att.mt_at <= out_step(q)) + 1
                    pe.wait_ge(s["mrow_ready"], rows)
                    for i in range(TPB):
                        last = nc.tensor.transpose(MI[:, i * P:(i + 1) * P], pvT[:, q % 2, i * P:(i + 1) * P],
                                                   ident[:, :])
                    last.then_inc(s["ot_done"], 1)

                for u in range(2 * att.units):
                    unit(u)
                maxima_to_rows(0)
                for t in range(att.steps + 2):
                    q, kt = t // att.kt, t % att.kt
                    if kt == att.mt_at and q + 1 < NQ:
                        maxima_to_rows(q + 1)
                    for h in range(QUAD):
                        if t < att.steps:
                            scores(t, h)
                        if q + 2 < NQ:
                            u0 = (q + 2) * att.units + kt * att.upb
                            for u in range(u0 + h * att.upb // QUAD, u0 + (h + 1) * att.upb // QUAD):
                                unit(u)
                    if 1 <= t <= att.steps:
                        values(t - 1)
                    if t >= 2 and (t - 2) % att.kt == att.kt - 1:
                        output_transposes((t - 2) // att.kt)

            pe.wait_ge(in_first, 16 * 5)
            project("proj_q0")
            project("proj_k0")
            pe.wait_ge(in_w, 16 * 7)
            project("proj_kc")
            context_values()
            pe.wait_ge(const_ready, 2)
            pe.wait_ge(ident_ready, 1)
            ring_empty("t_ln1")
            attention("a0")
            to_channels("t_ln1", norm_ready, 0, TPB)
            pe.wait_ge(fm_ready, 8)
            project("proj_q1")
            project("proj_k1")
            by_token("vals_s", w_sa, 2 * DIM)
            ring_empty("t_a1")
            attention("a1")
            to_channels("t_a1", ATT["a1"]["head_out"], NQ, 0)
            pe.wait_ge(fm_ready, 16)
            by_token("out_1", w_so, 0)
            to_channels("t_ln2", norm_ready, NT, TPB)
            pe.wait_ge(fm_ready, 24)
            project("proj_q2")
            ring_empty("t_a2")
            attention("a2")
            to_channels("t_a2", ATT["a2"]["head_out"], NQ, 0)
            pe.wait_ge(fm_ready, 32)
            by_token("out_2", w_co, 0)
            to_channels("t_ln3", norm_ready, 2 * NT, TPB)
            pe.wait_ge(fm_ready, 40)
            pe.wait_ge(in_ffn, 32)
            r = ring_at["ffn"]
            for tb in range(NB):
                for f in range(FF // P):
                    ps = bank(r)
                    for k in range(KC):
                        last = mm(ps, w_1[:, k, f * P:(f + 1) * P], fm[:, k, tb * BLK:(tb + 1) * BLK],
                                  start=(k == 0), stop=(k == KC - 1))
                    last.then_inc(mm_ready, 1)
                    r += 1
                for i in range(TPB):
                    ps = bank(r)
                    for f in range(FF // P):
                        if i == 0:
                            pe.wait_ge(hid_ready, tb * (FF // P) + f + 1)
                        last = mm(ps[:, 0:DIM], hid[:, f, i * P:(i + 1) * P], w_2[:, f, :],
                                  start=(f == 0), stop=(f == FF // P - 1))
                    last.then_inc(mm_ready, 1)
                    r += 1

        @block.scalar
        def _(act):
            act_fn = nc.scalar.activation
            with nc.allow_non_contiguous_dma("columns"):
                for c0, src, n in ((C_BQ0, bq0, 2), (C_BK0, bk0, 2), (C_SAQ, sa_b[0:DIM], 2),
                                   (C_SAK, sa_b[DIM:2 * DIM], 2), (C_CQ, cqb, 2), (C_CK, ckb, 2),
                                   (C_G1, g1, 2), (C_B1, b1n, 2), (C_G2, g2, 2), (C_B2, b2n, 2),
                                   (C_G3, g3, 2), (C_B3, b3n, 2), (C_F1, b1, 8)):
                    act.dma_start(cols[:, c0:c0 + n], src.rearrange("(k p) -> p k", p=P)).then_inc(in_b, 16)
                for n, src in ((B_V0, bv0), (B_VS, sa_b[2 * DIM:]), (B_SO, so_b), (B_CV, cvb), (B_CO, cob),
                               (B_F2, b2)):
                    act.dma_start(bc[:, n, :], src.partition_broadcast(P)).then_inc(in_b, 16)
            act.wait_ge(in_b, 16 * 19)
            act.wait_ge(bias_scaled, 1)

            def split_first(name):
                for spec, n, r, mc, _c0, width in split_chunks(name):
                    act.wait_ge(mm_ready, r + 1)
                    if n >= 2:
                        act.wait_ge(rest1_ready, n - 1)
                    act_fn(q32[:, n % 2, 0:width], ring[r % BPR][:, 0:width], ACT.Identity,
                           bias=cols[:, spec[3] + mc:spec[3] + mc + 1], scale=spec[4]) \
                        .then_inc(q32_ready, 1)
                    act.wait_ge(q32_ready, n + 1)
                    if n >= 2:
                        act.wait_ge(parts_stored[n % 2], 16 * (n // 2))
                    act_fn(split[:, n % 2, 0, 0:width], q32[:, n % 2, 0:width], ACT.Copy) \
                        .then_inc(part1_ready, 1)

            def channels_out(name, first, gain=None, bias=None):
                for n in range(NB * KC):
                    r, tb, c = ring_at[name] + n, n // KC, n % KC
                    act.wait_ge(mm_ready, r + 1)
                    dst = fm[:, c, tb * BLK:(tb + 1) * BLK]
                    if gain is None:
                        ins = act_fn(dst, ring[r % BPR], ACT.Copy)
                    else:
                        ins = act_fn(dst, ring[r % BPR], ACT.Identity, bias=cols[:, bias + c:bias + c + 1],
                                     scale=cols[:, gain + c:gain + c + 1])
                    ins.then_inc(fm_ready, 1)

            def attention(name):
                att, *_r = SPEC[name]
                s = ATT[name]

                def maxima_out(q):
                    act.wait_ge(s["mt_done"], q + 1)
                    if q >= 2:
                        act.wait_ge(s["rows_in"][q % 2], 16 * PARTS * (q // 2))
                    act_fn(mrow[:, q % 2, :], MIb[0:PARTS * QUAD, 0:BLK], ACT.Copy).then_inc(s["mrow_ready"], 1)

                maxima_out(0)
                for t in range(att.steps + 1):
                    q, kt = t // att.kt, t % att.kt
                    if kt == att.mt_at and q + 1 < NQ and not att.whole:
                        maxima_out(q + 1)
                    if t < att.steps:
                        if t >= 2:
                            act.wait_ge(s["pv_done"], t - 1)
                        for h in range(QUAD):
                            n = t * QUAD + h
                            act.wait_ge(s["st_done"], n + 1)
                            act_fn(prob[0:att.keys, t % 2, h, :], ST[0:att.keys, n % 2, :], ACT.Exp) \
                                .then_inc(s["exp_done"], 1)
                    if kt == att.mt_at and q + 1 < NQ and att.whole:
                        maxima_out(q + 1)
                    if t >= 1 and t % att.kt == 0:
                        qq = t // att.kt - 1
                        act.wait_ge(s["pv_done"], t)
                        if qq >= 2:
                            act.wait_ge(s["ot_done"], qq - 1)
                        act_fn(pvT[:, qq % 2, :], PV[:, :], ACT.Copy).then_inc(s["pv_out"], 1)

            split_first("proj_q0")
            split_first("proj_k0")
            split_first("proj_kc")
            attention("a0")
            channels_out("t_ln1", 0, C_G1, C_B1)
            split_first("proj_q1")
            split_first("proj_k1")
            attention("a1")
            channels_out("t_a1", 8)
            channels_out("t_ln2", 16, C_G2, C_B2)
            split_first("proj_q2")
            attention("a2")
            channels_out("t_a2", 24)
            channels_out("t_ln3", 32, C_G3, C_B3)
            r = ring_at["ffn"]
            for tb in range(NB):
                if tb >= 1:
                    act.wait_ge(mm_ready, r)
                for f in range(FF // P):
                    act.wait_ge(mm_ready, r + 1)
                    act_fn(hid[:, f, :], ring[r % BPR], ACT.Gelu, bias=cols[:, C_F1 + f:C_F1 + f + 1]) \
                        .then_inc(hid_ready, 1)
                    r += 1
                r += TPB

        @block.vector
        def _(dve):
            vec = nc.vector

            def split_rest(name):
                for spec, n, r, mc, _c0, width in split_chunks(name):
                    dve.wait_ge(part1_ready, n + 1)
                    vec.tensor_tensor(r32[:, n % 2, 0:width], q32[:, n % 2, 0:width],
                                      split[:, n % 2, 0, 0:width], ALU.subtract).then_inc(rest1_ready, 1)
                    dve.wait_ge(rest1_ready, n + 1)
                    vec.tensor_copy(split[:, n % 2, 1, 0:width], r32[:, n % 2, 0:width]) \
                        .then_inc(part2_ready, 1)
                    dve.wait_ge(part2_ready, n + 1)
                    vec.tensor_tensor(split[:, n % 2, 2, 0:width], r32[:, n % 2, 0:width],
                                      split[:, n % 2, 1, 0:width], ALU.subtract).then_inc(parts_ready, 1)

            def attention(name):
                att, *_r = SPEC[name]
                s = ATT[name]

                def unit(u):
                    q, v = u // att.units, u % att.units
                    dve.wait_ge(s["sm_done"], u + 1)
                    if v == 0 and q >= 2:
                        dve.wait_ge(s["mp_ready"], q - 1)
                    if att.whole:
                        qt, h = v // QUAD, v % QUAD
                        vec.tensor_reduce(nm[:, q % 2, qt, h:h + 1], SM[:, u % 2, :], AX.X, ALU.max,
                                          negate=True).then_inc(s["max_done"], 1)
                    else:
                        src = SM[:, u % 2, 0:QUAD * att.keys].rearrange("p (h k) -> p h k", h=QUAD)
                        vec.tensor_reduce(nm[:, q % 2, v, :], src, AX.X, ALU.max,
                                          negate=True).then_inc(s["max_done"], 1)

                def output(q):
                    g, j = q // HALVES, q % HALVES
                    b, h0 = g // QUAD, (g % QUAD) * QUAD
                    t0 = b * (SEQ // P) + j * TPB
                    heads = MI[:, :].rearrange("p (i h c) -> p i h c", i=TPB, h=QUAD)
                    dve.wait_ge(s["ot_done"], q + 1)
                    vec.reciprocal(rden[:, q % 2], heads[:, :, :, HD:HD + 1].rearrange("p i h c -> p i (h c)")) \
                        .then_inc(s["rd_done"], 1)
                    dve.wait_ge(s["rd_done"], q + 1)
                    dst = A[:, t0:t0 + TPB, h0 * HD:(h0 + QUAD) * HD].rearrange("p i (h d) -> p i h d", h=QUAD)
                    vec.tensor_tensor(dst, heads[:, :, :, 0:HD],
                                      rden[:, q % 2].unsqueeze(3).to_broadcast([P, TPB, QUAD, HD]),
                                      ALU.mult).then_inc(s["head_out"], 1)

                for u in range(2 * att.units):
                    unit(u)
                for t in range(att.steps + 2):
                    q, kt = t // att.kt, t % att.kt
                    if q + 2 < NQ:
                        u0 = (q + 2) * att.units + kt * att.upb
                        for u in range(u0, u0 + att.upb):
                            unit(u)
                    if t >= 2 and (t - 2) % att.kt == att.kt - 1:
                        output((t - 2) // att.kt)

            def norm(n, x_at):
                for t in range(NT):
                    if x_at is not None:
                        dve.wait_ge(x_ready, x_at + t + 1)
                    vec.bn_stats(stats[:, t, :], X[:, t, :]).then_inc(stat_ready, 1)
                    dve.wait_ge(stat_ready, n * NT + t + 1)
                    vec.bn_aggr(mv[:, t, :], stats[:, t, :]).then_inc(mv_ready, 1)
                dve.wait_ge(rstd_ready, n + 1)
                for t in range(NT):
                    vec.tensor_scalar(A[:, t, :], X[:, t, :], mv[:, t, 0:1], rstd[:, t:t + 1],
                                      ALU.subtract, ALU.mult).then_inc(norm_ready, 1)

            dve.wait_ge(in_b, 16 * 19)
            for n, c in enumerate((C_BQ0, C_SAQ, C_CQ)):
                ins = vec.tensor_scalar(cols[:, c:c + 2], cols[:, c:c + 2], SCALE, None, ALU.mult)
            ins.then_inc(bias_scaled, 1)
            dve.wait_ge(in_first, 16 * 5)
            vec.tensor_copy(identb[:, :], ident[:, :]).then_inc(ident_ready, 1)
            split_rest("proj_q0")
            split_rest("proj_k0")
            split_rest("proj_kc")
            for a in range(2):
                for b in range(BATCH):
                    r = ring_at["vals_c"] + 2 * a + b
                    dve.wait_ge(mm_ready, r + 1)
                    vec.tensor_tensor(Vc[0:CTX, a, b, :], ring[r % BPR][0:CTX, 0:DIM],
                                      bc[0:CTX, B_V0 if a == 0 else B_CV, :], ALU.add).then_inc(v_ready, 1)
            attention("a0")
            dve.wait_ge(in_x, 16)
            dve.wait_ge(ATT["a0"]["head_out"], NQ)
            for t in range(NT):
                vec.tensor_tensor(X[:, t, :], X[:, t, :], A[:, t, :], ALU.add).then_inc(x_ready, 1)
            norm(0, 0)
            split_rest("proj_q1")
            split_rest("proj_k1")
            for t in range(NT):
                r = ring_at["vals_s"] + t
                dve.wait_ge(mm_ready, r + 1)
                vec.tensor_tensor(V[:, t, :], ring[r % BPR][:, 0:DIM], bc[:, B_VS, :], ALU.add).then_inc(v_ready, 1)
            attention("a1")
            dve.wait_ge(bias_added, 1)
            for t in range(NT):
                r = ring_at["out_1"] + t
                dve.wait_ge(mm_ready, r + 1)
                vec.tensor_tensor(X[:, t, :], ring[r % BPR][:, 0:DIM], X[:, t, :], ALU.add).then_inc(x_ready, 1)
            norm(1, NT)
            split_rest("proj_q2")
            attention("a2")
            dve.wait_ge(bias_added, 2)
            for t in range(NT):
                r = ring_at["out_2"] + t
                dve.wait_ge(mm_ready, r + 1)
                vec.tensor_tensor(X[:, t, :], ring[r % BPR][:, 0:DIM], X[:, t, :], ALU.add).then_inc(x_ready, 1)
            norm(2, 2 * NT)
            dve.wait_ge(bias_added, 3)
            for tb in range(NB):
                for i in range(TPB):
                    r = ring_at["ffn"] + tb * 12 + 8 + i
                    dve.wait_ge(mm_ready, r + 1)
                    t = tb * TPB + i
                    vec.tensor_tensor(X[:, t, :], ring[r % BPR][:, 0:DIM], X[:, t, :], ALU.add).then_inc(x_ready, 1)

        @block.gpsimd
        def _(pool):
            gp = nc.gpsimd
            gp.memset(stacks[SROWS:P, :, 0, :, :], 1.0).then_inc(const_ready, 1)
            pool.wait_ge(const_ready, 1)
            gp.memset(Vst[:, :, :, :, :], 0.0).then_inc(var_ready, 1)
            pool.wait_ge(var_ready, 1)
            gp.memset(Vst[:, :, :, :, HD:HD + 1], 1.0).then_inc(const_ready, 1)
            gp.memset(nexp[:, :], -0.5).then_inc(var_ready, 1)

            def attention(name):
                att, _q, _k, vc = SPEC[name]
                s = ATT[name]

                def stationary(g):
                    b, h0 = g // QUAD, (g % QUAD) * QUAD
                    if g >= 2:
                        pool.wait_ge(s["pv_done"], (g - 1) * HALVES * att.kt)
                    if att.whole:
                        src = V[:, b * att.kt:(b + 1) * att.kt, h0 * HD:(h0 + QUAD) * HD]
                        gp.tensor_copy(Vst[:, g % 2, :, :, 0:HD], src.rearrange("p k (h d) -> p k h d", h=QUAD)) \
                            .then_inc(s["vst_ready"], 1)
                    else:
                        src = vc[0:CTX, b, h0 * HD:(h0 + QUAD) * HD]
                        gp.tensor_copy(Vst[0:CTX, g % 2, 0, :, 0:HD], src.rearrange("p (h d) -> p h d", h=QUAD)) \
                            .then_inc(s["vst_ready"], 1)

                def parts_of_maxima(q):
                    pool.wait_ge(s["max_done"], (q + 1) * att.units)
                    if q >= 2:
                        pool.wait_ge(s["mt_done"], q - 1)
                    a, r, m = nm[:, q % 2], nr[:, q % 2], mp[:, q % 2]
                    gp.tensor_copy(m[:, :, 0, :], a).then_inc(s["mp_p1"], 1)
                    pool.wait_ge(s["mp_p1"], q + 1)
                    gp.tensor_tensor(r, a, m[:, :, 0, :], ALU.subtract).then_inc(s["mp_r1"], 1)
                    pool.wait_ge(s["mp_r1"], q + 1)
                    gp.tensor_copy(m[:, :, 1, :], r).then_inc(s["mp_p2"], 1)
                    pool.wait_ge(s["mp_p2"], q + 1)
                    gp.tensor_tensor(m[:, :, 2, :], r, m[:, :, 1, :], ALU.subtract).then_inc(s["mp_ready"], 1)

                stationary(0)
                stationary(1)
                parts_of_maxima(0)
                parts_of_maxima(1)
                for q in range(NQ - 2):
                    if q >= 2 and q % 2 == 0:
                        stationary(q // 2 + 1)
                    parts_of_maxima(q + 2)

            def rsqrt(n):
                pool.wait_ge(mv_ready, (n + 1) * NT)
                gp.tensor_scalar(rstd[:, :], mv[:, :, 1], EPS, None, ALU.add).then_inc(var_ready, 1)
                pool.wait_ge(var_ready, 3 + n)
                gp.tensor_tensor(rstd[:, :], rstd[:, :], nexp[:, :], ALU.pow).then_inc(rstd_ready, 1)

            def add_bias(n, which, after_norm):
                pool.wait_ge(norm_ready, NT * after_norm)
                for t in range(NT):
                    ins = gp.tensor_tensor(X[:, t, :], X[:, t, :], bc[:, which, :], ALU.add)
                ins.then_inc(bias_added, 1)

            pool.wait_ge(v_ready, 4)
            attention("a0")
            rsqrt(0)
            add_bias(0, B_SO, 1)
            pool.wait_ge(v_ready, 4 + NT)
            attention("a1")
            rsqrt(1)
            add_bias(1, B_CO, 2)
            attention("a2")
            rsqrt(2)
            add_bias(2, B_F2, 3)


def kernel(**inputs):
    import numpy as _np
    import concourse.bacc as _bacc
    from concourse import mybir as _mybir
    from concourse.bass_utils import run_bass_kernel_spmd as _run

    g = {k: _np.asarray(v) for k, v in inputs.items()}
    x = g["x"].reshape(TOK, DIM)
    c = g["ctx_1024"].reshape(BATCH * CTX, DIM)
    L0 = {k[9:]: v for k, v in g.items() if k.startswith("L0_xattn_")}
    L1 = {k[9:]: v for k, v in g.items() if k.startswith("L1_xattn_")}
    arrays = [
        ("xT", x.T), ("x", x), ("ctxT", c.T), ("ident", _np.eye(P, dtype=_np.float32)),
        ("wq0", L0["Wq"]), ("bq0", L0["bq"]), ("wk0", L0["Wk"]), ("bk0", L0["bk"]),
        ("wv0", L0["Wv"]), ("bv0", L0["bv"]),
        ("sa_w", L1["sa_in_w"].T), ("sa_b", L1["sa_in_b"]), ("so_w", L1["sa_out_w"].T), ("so_b", L1["sa_out_b"]),
        ("g1", L1["ln1_g"]), ("b1n", L1["ln1_b"]), ("cqw", L1["cq_w"].T), ("cqb", L1["cq_b"]),
        ("ckw", L1["ck_w"].T), ("ckb", L1["ck_b"]), ("cvw", L1["cv_w"].T), ("cvb", L1["cv_b"]),
        ("cow", L1["co_w"].T), ("cob", L1["co_b"]), ("g2", L1["ln2_g"]), ("b2n", L1["ln2_b"]),
        ("w1", L1["w1"].T), ("b1", L1["b1"]), ("w2", L1["w2"].T), ("b2", L1["b2"]),
        ("g3", L1["ln3_g"]), ("b3n", L1["ln3_b"]),
    ]
    nc = _bacc.Bacc("TRN2", target_bir_lowering=False, num_devices=1)
    feeds, args = {}, []
    for name, a in arrays:
        a = _np.ascontiguousarray(a)
        feeds[f"in_{name}"] = a
        args.append(nc.dram_tensor(f"in_{name}", a.shape, _mybir.dt.from_np(a.dtype), kind="ExternalInput").ap())
    args.append(nc.dram_tensor("out_0", (TOK, DIM), _mybir.dt.float32, kind="ExternalOutput").ap())
    xattn_kernel(nc, *args)
    r = _run(nc, [feeds], core_ids=[0])
    return r.results[0]["out_0"].reshape(BATCH, SEQ, DIM)
```

```python
import concourse.bass as bass
from concourse import mybir
from contextlib import ExitStack

FP32 = mybir.dt.float32
BF16 = mybir.dt.bfloat16
ALU = mybir.AluOpType
ACT = mybir.ActivationFunctionType
AX = mybir.AxisListType

BATCH, SEQ, DIM = 2, 1024, 256
HEADS = 16
HD = DIM // HEADS
CTX = 77
TOK = BATCH * SEQ
FF = 1024
EPS = 1e-5
SCALE = HD ** -0.5

P = 128
KC = DIM // P
NT = TOK // P
BLK = 512
NB = TOK // BLK
TPB = BLK // P
QUAD = 4
NG = BATCH * HEADS // QUAD
HALVES = SEQ // BLK
NQ = NG * HALVES
PARTS = 3
BANDS = [(0, 0), (0, 1), (0, 2), (1, 0), (1, 1), (2, 0)]
SROWS = len(BANDS) * HD
MROWS = SROWS + PARTS
SB = 4


class Attention:

    def __init__(self, key_tiles, keys, ahead, rows_ahead, buffers, banks):
        self.kt = key_tiles
        self.keys = keys
        self.steps = NQ * key_tiles
        self.whole = key_tiles > 1
        self.units = TPB * (QUAD if self.whole else 1)
        self.ahead = ahead
        self.rows_ahead = rows_ahead
        self.buffers = buffers
        self.banks = banks
        self.before = [("max", u) for u in range(ahead * self.units)] + [("rows", q) for q in range(rows_ahead)]
        self.at = {}
        order = self.before + [x[1:] for t in range(self.steps + 2) for x in self.side(t)]
        for i, what in enumerate(order):
            self.at[what] = i

    def side(self, t):
        q, kt = divmod(t, self.kt)
        work = []
        if q + self.ahead < NQ:
            n = self.units // self.kt
            u0 = (q + self.ahead) * self.units + kt * n
            work += [((i + 1) * QUAD // n - 1, "max", u0 + i) for i in range(n)]
        if kt == (1 if self.whole else 0) and q + self.rows_ahead < NQ:
            work.append((2, "rows", q + self.rows_ahead))
        if t >= 2 and (t - 2) % self.kt == self.kt - 1:
            work.append((3, "out", (t - 2) // self.kt))
        return sorted(work, key=lambda w: w[0])

    def read(self, kind, which):
        return self.at[kind, which] + 1


SELF = Attention(SEQ // P, P, ahead=2, rows_ahead=1, buffers=3, banks=2)
CROSS = Attention(1, CTX, ahead=3, rows_ahead=2, buffers=4, banks=4)


def xattn_kernel(nc, xT_d, x_d, cT_d, ident_d, wq0, bq0, wk0, bk0, wv0, bv0,
                 sa_w, sa_b, so_w, so_b, g1, b1n, cqw, cqb, ckw, ckb, cvw, cvb, cow, cob,
                 g2, b2n, w1, b1, w2, b2, g3, b3n, out):
    q_parts = nc.dram_tensor("q_parts", [3, PARTS, BATCH * DIM, SEQ], BF16).ap()
    k_parts = nc.dram_tensor("k_parts", [PARTS, BATCH * DIM, SEQ], BF16).ap()
    c_parts = nc.dram_tensor("c_parts", [2, PARTS, DIM, BATCH * CTX], BF16).ap()

    ctx = ExitStack()
    with ctx:
        def sb(name, shape, dt=FP32):
            return ctx.enter_context(nc.sbuf_tensor(name, shape, dt))

        def sem(name):
            return ctx.enter_context(nc.semaphore(name))

        fm = sb("fm", [P, KC, TOK])
        X = sb("X", [P, NT, DIM])
        A = sb("A", [P, NT, DIM])
        V = sb("V", [P, NG, SEQ // P, QUAD * HD])
        w_q0 = sb("w_q0", [P, KC, DIM]); w_k0 = sb("w_k0", [P, KC, DIM]); w_v0 = sb("w_v0", [P, KC, DIM])
        w_sa = sb("w_sa", [P, KC, 3 * DIM]); w_so = sb("w_so", [P, KC, DIM])
        w_cq = sb("w_cq", [P, KC, DIM]); w_ck = sb("w_ck", [P, KC, DIM])
        w_cv = sb("w_cv", [P, KC, DIM]); w_co = sb("w_co", [P, KC, DIM])
        w_1 = V[:, 0:NG // 2].rearrange("p a b c -> p (a b c)").rearrange("p (k f) -> p k f", k=KC)
        w_2 = V[:, NG // 2:NG].rearrange("p a b c -> p (a b c)").rearrange("p (k f) -> p k f", k=FF // P)
        ctxT = sb("ctxT", [P, KC, BATCH * CTX])
        Vc = sb("Vc", [P, 2, BATCH, DIM])
        stacks = sb("stacks", [P, SELF.buffers, 2, QUAD, SEQ], BF16)
        Kst = [stacks[:, n, 0] for n in range(SELF.buffers)]
        Kc = stacks[:, 0, 0].rearrange("p h t -> p (h t)")[:, 0:HEADS * BATCH * CTX] \
            .rearrange("p (h t) -> p h t", h=HEADS)
        Qst = [stacks[:, n, 1] for n in range(SELF.buffers)] + [Kst[1]]
        Vst = sb("Vst", [P, 2, SELF.kt, QUAD, 32])
        prob = sb("prob", [P, 2, QUAD, BLK])
        hid = [stacks[:, n].rearrange("p a h t -> p (a h t)").bitcast(FP32)
               .rearrange("p (f t) -> p f t", f=FF // P) for n in range(2)]
        pvT = sb("pvT", [P, 2, BLK])
        q32 = sb("q32", [P, SB, BLK])
        r32 = sb("r32", [P, SB, BLK])
        split = sb("split", [P, SB, PARTS, BLK], BF16)
        mrow = sb("mrow", [PARTS * QUAD, 2, BLK], BF16)
        nm = sb("nm", [P, 2, TPB, QUAD])
        nr = sb("nr", [P, 2, TPB, QUAD])
        mp = sb("mp", [P, 2, TPB, PARTS, QUAD], BF16)
        rden = sb("rden", [P, 2, TPB, QUAD])
        ident = sb("ident", [P, P])
        identb = sb("identb", [P, P], BF16)
        cols = sb("cols", [P, 40])
        bc = sb("bc", [P, 6, DIM])
        stats = sb("stats", [P, NT, 6])
        mv = sb("mv", [P, NT, 2])
        rstd = sb("rstd", [P, NT])
        nexp = sb("nexp", [P, NT])

        SM = ctx.enter_context(nc.psum_tensor("SM", [P, 4, BLK], FP32))
        ST = ctx.enter_context(nc.psum_tensor("ST", [P, 3, BLK], FP32))
        PV = ctx.enter_context(nc.psum_tensor("PV", [P, BLK], FP32))
        ring = [ST[:, 0, :], ST[:, 1, :], ST[:, 2, :], PV[:, :]]

        def side_bank(att, i):
            n = 4 // att.banks
            k = i % att.banks
            return SM[:, k * n:(k + 1) * n, :].rearrange("p n c -> p (n c)")

        def values_of(t):
            b, i = divmod(t, SEQ // P)
            return V[:, b * QUAD:(b + 1) * QUAD, i, :]

        C_BQ0, C_BK0, C_SAQ, C_SAK, C_CQ, C_CK = 0, 2, 4, 6, 8, 10
        C_G1, C_B1, C_G2, C_B2, C_G3, C_B3, C_F1 = 12, 14, 16, 18, 20, 22, 24
        B_V0, B_VS, B_SO, B_CV, B_CO, B_F2 = range(6)

        in_ctx = sem("in_ctx")
        in_xT = [sem(f"in_xT{n}") for n in range(NB)]
        in_x = sem("in_x")
        in_w = sem("in_w")
        in_b = sem("in_b")
        in_ffn = sem("in_ffn")
        const_ready = sem("const_ready")
        ident_ready = sem("ident_ready")
        bias_scaled = sem("bias_scaled")
        out_done = sem("out_done")
        in_counts = {}

        mm_ready = sem("mm_ready")
        q32_ready = sem("q32_ready"); part1_ready = sem("part1_ready"); rest1_ready = sem("rest1_ready")
        part2_ready = sem("part2_ready"); parts_ready = sem("parts_ready")
        parts_stored = [sem(f"parts_stored{n}") for n in range(SB)]
        fm_ready = sem("fm_ready")
        stat_ready = sem("stat_ready"); mv_ready = sem("mv_ready"); rstd_ready = sem("rstd_ready")
        norm_ready = sem("norm_ready")
        x_ready = [sem(f"x{n}_ready") for n in range(4)]
        v_ready = sem("v_ready")
        bias_added = sem("bias_added")
        hid_ready = sem("hid_ready")
        var_ready = sem("var_ready")
        pool_step = sem("pool_step")

        BPR = len(ring)
        PER = {"proj_q0": 2, "proj_k0": 2, "proj_kc": 2, "vals_c": 4, "t_ln1": 2, "proj_q1": 2,
               "proj_k1": 2, "vals_s": 4, "t_a1": 2, "out_1": 4, "t_ln2": 2, "proj_q2": 2,
               "t_a2": 2, "out_2": 4, "t_ln3": 2, "up": 8, "down": 4}
        BEFORE_A0 = [("proj_k0", 0), ("proj_kc", 0), ("vals_c", 0)] + [("proj_q0", tb) for tb in range(NB)]
        BEFORE_A1 = [(stage, tb) for tb in range(2) for stage in ("t_ln1", "proj_q1", "proj_k1", "vals_s")]
        for tb in (2, 3):
            for n, stage in enumerate(("t_ln1", "proj_q1", "proj_k1", "vals_s")):
                BEFORE_A1 += [(stage, tb), ("side", 4 * (tb - 2) + n)]
        BEFORE_A2 = [("t_a1", 0), ("out_1", 0), ("t_a1", 1), ("out_1", 1), ("t_ln2", 0), ("proj_q2", 0),
                     ("t_a1", 2), ("out_1", 2), ("t_ln2", 1), ("proj_q2", 1), ("t_a1", 3), ("out_1", 3),
                     ("t_ln2", 2), ("proj_q2", 2), ("t_ln2", 3), ("proj_q2", 3)]
        AFTER_A2 = [("t_a2", 0), ("out_2", 0), ("t_a2", 1), ("out_2", 1), ("t_ln3", 0), ("up", 0),
                    ("t_a2", 2), ("out_2", 2), ("t_ln3", 1), ("up", 1), ("down", 0), ("t_a2", 3),
                    ("out_2", 3), ("t_ln3", 2), ("up", 2), ("down", 1), ("t_ln3", 3), ("up", 3),
                    ("down", 2), ("down", 3)]
        SPLITS = {
            "proj_q0": (w_q0, 0, C_BQ0, SCALE, "x", q_parts[0]),
            "proj_k0": (w_k0, 0, C_BK0, 1.0, "c", c_parts[0]),
            "proj_kc": (w_ck, 0, C_CK, 1.0, "c", c_parts[1]),
            "proj_q1": (w_sa, 0, C_SAQ, SCALE, "x", q_parts[1]),
            "proj_k1": (w_sa, DIM, C_SAK, 1.0, "x", k_parts),
            "proj_q2": (w_cq, 0, C_CQ, SCALE, "x", q_parts[2]),
        }
        READER = {"vals_c": v_ready, "vals_s": v_ready, "out_1": x_ready[1], "out_2": x_ready[2],
                  "down": x_ready[3], "up": hid_ready}
        RING, READ, COUNT = {}, [], {}
        for stage, tb in BEFORE_A0 + BEFORE_A1 + BEFORE_A2 + AFTER_A2:
            if stage == "side":
                continue
            who = q32_ready if stage in SPLITS else fm_ready if stage[:2] == "t_" else READER[stage]
            for i in range(PER[stage]):
                COUNT[who.name] = COUNT.get(who.name, 0) + 1
                RING[stage, tb, i] = len(READ)
                READ.append((who, COUNT[who.name]))

        def chunks(stage, tb):
            for mc in range(KC):
                r = RING[stage, tb, mc]
                width = BLK if SPLITS[stage][4] == "x" else BATCH * CTX
                yield READ[r][1] - 1, r, mc, tb * BLK, width

        def fm_count(stage, tb):
            return READ[RING[stage, tb, KC - 1]][1]

        def stored(eng, stage, tb):
            upto = READ[RING[stage, tb, KC - 1]][1]
            for k in range(SB):
                eng.wait_ge(parts_stored[k], 16 * len(range(k, upto, SB)))

        pad_ready = sem("pad_ready")
        ATT = {}
        for name in ("a0", "a1", "a2"):
            s = ATT[name] = {}
            for what in ("side_done",
                         "side_read",
                         "mp_p1", "mp_r1", "mp_p2", "mp_ready",
                         "st_done", "exp_done", "pv_done",
                         "pv_out",
                         "rd_done", "vst_ready"):
                s[what] = sem(f"{name}_{what}")
            s["keys_in"] = sem(f"{name}_keys_in")
            s["stack_in"] = [sem(f"{name}_stack{n}") for n in range(CROSS.buffers)]
            s["rows_in"] = [sem(f"{name}_rows{n}") for n in range(2)]
        SPEC = {"a0": (CROSS, q_parts[0], c_parts[0], Vc[:, 0]),
                "a1": (SELF, q_parts[1], k_parts, None),
                "a2": (CROSS, q_parts[2], c_parts[1], Vc[:, 1])}
        NSD = len(BANDS)

        def last_half(tb):
            return (tb // HALVES) * (NQ // BATCH) + (QUAD - 1) * HALVES + tb % HALVES

        block = ctx.enter_context(nc.Block())

        @block.sync
        def _(sp):
            sp.dma_start(ctxT[:, :, :], cT_d.rearrange("(k p) t -> p k t", p=P)).then_inc(in_ctx, 16)
            sp.dma_start(w_k0[:, :, :], wk0.rearrange("(k p) n -> p k n", p=P)).then_inc(in_ctx, 16)
            for tile, src in ((w_ck, ckw), (w_v0, wv0), (w_cv, cvw), (w_q0, wq0)):
                sp.dma_start(tile[:, :, :], src.rearrange("(k p) n -> p k n", p=P)).then_inc(in_ctx, 16)
            for tb in range(NB):
                cols_tb = slice(tb * BLK, (tb + 1) * BLK)
                sp.dma_start(fm[:, :, cols_tb], xT_d[:, cols_tb].rearrange("(k p) t -> p k t", p=P)) \
                  .then_inc(in_xT[tb], 16)
            sp.dma_start(ident[:, :], ident_d).then_inc(in_w, 16)
            for tile, src in ((w_sa, sa_w), (w_so, so_w), (w_cq, cqw), (w_co, cow)):
                sp.dma_start(tile[:, :, :], src.rearrange("(k p) n -> p k n", p=P)).then_inc(in_w, 16)
            sp.dma_start(X[:, :, :], x_d.rearrange("(t p) d -> p t d", p=P)).then_inc(in_x, 16)

            def store_parts(stage, tb):
                for n, _r, mc, c0, width in chunks(stage, tb):
                    sp.wait_ge(parts_ready, n + 1)
                    if SPLITS[stage][4] == "x":
                        b, c = divmod(c0, SEQ)
                        dst = SPLITS[stage][5][:, b * DIM + mc * P:b * DIM + (mc + 1) * P, c:c + width]
                    else:
                        dst = SPLITS[stage][5][:, mc * P:(mc + 1) * P, :]
                    sp.dma_start(dst.rearrange("r p t -> p r t"), split[:, n % SB, :, 0:width]) \
                      .then_inc(parts_stored[n % SB], 16)

            def stack(name, g):
                att, qp, kp, _v = SPEC[name]
                s = ATT[name]
                n = g % att.buffers
                if g >= att.buffers:
                    sp.wait_ge(s["st_done"], (g - att.buffers + 1) * HALVES * att.kt * QUAD)
                heads = slice(g * QUAD * HD, (g + 1) * QUAD * HD)
                for band, (kpart, qpart) in enumerate(BANDS):
                    rows = slice(band * HD, (band + 1) * HD)
                    if att.whole:
                        sp.dma_start(Kst[n][rows, :, :], kp[kpart, heads, :].rearrange("(h d) t -> d h t", d=HD)) \
                          .then_inc(s["stack_in"][n], 16)
                    sp.dma_start(Qst[n][rows, :, :], qp[qpart, heads, :].rearrange("(h d) t -> d h t", d=HD)) \
                      .then_inc(s["stack_in"][n], 16)

            def context_keys(name):
                _att, _qp, kp, _v = SPEC[name]
                for band, (kpart, _qpart) in enumerate(BANDS):
                    sp.dma_start(Kc[band * HD:(band + 1) * HD, :, :], kp[kpart].rearrange("(h d) t -> d h t", d=HD)) \
                      .then_inc(ATT[name]["keys_in"], 16)

            def maxima(name, q):
                att, *_r = SPEC[name]
                s = ATT[name]
                g, j = q // HALVES, q % HALVES
                sp.wait_ge(s["side_read"], att.read("rows", q))
                sp.dma_start(Qst[g % att.buffers][SROWS:MROWS, :, j * BLK:(j + 1) * BLK], mrow[:, q % 2, :]) \
                  .then_inc(s["rows_in"][q % 2], 16)

            def attention(name, stage):
                att, *_r = SPEC[name]
                for q in range(att.rows_ahead):
                    maxima(name, q)
                for q in range(NQ - att.rows_ahead):
                    g = q // HALVES + att.buffers - 1
                    if q % 2 == 0 and g < NG:
                        if g == QUAD:
                            stored(sp, stage, NB - 1)
                        stack(name, g)
                    maxima(name, q + att.rows_ahead)

            store_parts("proj_k0", 0)
            store_parts("proj_kc", 0)
            stored(sp, "proj_kc", 0)
            sp.wait_ge(pad_ready, 1)
            context_keys("a0")
            store_parts("proj_q0", 0)
            store_parts("proj_q0", 1)
            stored(sp, "proj_q0", 1)
            for g in range(CROSS.buffers - 1):
                stack("a0", g)
            store_parts("proj_q0", 2)
            store_parts("proj_q0", 3)
            attention("a0", "proj_q0")
            for tb in range(NB):
                store_parts("proj_q1", tb)
                store_parts("proj_k1", tb)
                if tb == 1:
                    stored(sp, "proj_k1", 1)
                    for g in range(SELF.buffers - 1):
                        stack("a1", g)
            attention("a1", "proj_k1")
            sp.wait_ge(ATT["a1"]["vst_ready"], NG)
            sp.dma_start(w_1, w1.rearrange("(k p) n -> p k n", p=P)).then_inc(in_ffn, 16)
            sp.dma_start(w_2, w2.rearrange("(k p) n -> p k n", p=P)).then_inc(in_ffn, 16)
            sp.wait_ge(ATT["a1"]["st_done"], SELF.steps * QUAD)
            sp.wait_ge(pad_ready, 3)
            context_keys("a2")
            for tb in range(NB):
                store_parts("proj_q2", tb)
                if tb == 1:
                    stored(sp, "proj_q2", 1)
                    for g in range(CROSS.buffers - 1):
                        stack("a2", g)
            attention("a2", "proj_q2")
            for t in range(NT):
                sp.wait_ge(x_ready[3], t + 1)
                sp.dma_start(out[t * P:(t + 1) * P, :], X[:, t, :]).then_inc(out_done, 16)
            sp.wait_ge(out_done, 16 * NT)

        @block.tensor
        def _(pe):
            mm = nc.tensor.matmul

            def bank(stage, tb, i):
                r = RING[stage, tb, i]
                if r >= BPR:
                    pe.wait_ge(*READ[r - BPR])
                return ring[r % BPR]

            def ring_empty(last_stage, tb):
                last = RING[last_stage, tb, PER[last_stage] - 1]
                for r in range(last + 1 - BPR, last + 1):
                    pe.wait_ge(*READ[r])

            def project(stage, tb):
                w, w0, _b, _s, source, _st = SPLITS[stage]
                src = fm if source == "x" else ctxT
                for _n, r, mc, c0, width in chunks(stage, tb):
                    ps = bank(stage, tb, mc)
                    for k in range(KC):
                        last = mm(ps[:, 0:width], w[:, k, w0 + mc * P:w0 + (mc + 1) * P],
                                  src[:, k, c0:c0 + width], start=(k == 0), stop=(k == KC - 1))
                    last.then_inc(mm_ready, 1)

            def context_values():
                for a, w in enumerate((w_v0, w_cv)):
                    for b in range(BATCH):
                        ps = bank("vals_c", 0, a * BATCH + b)
                        for k in range(KC):
                            last = mm(ps[0:CTX, 0:DIM], ctxT[:, k, b * CTX:(b + 1) * CTX], w[:, k, :],
                                      start=(k == 0), stop=(k == KC - 1))
                        last.then_inc(mm_ready, 1)

            def to_channels(stage, tb):
                for c in range(KC):
                    ps = bank(stage, tb, c)
                    for i in range(TPB):
                        last = nc.tensor.transpose(ps[:, i * P:(i + 1) * P],
                                                   A[:, tb * TPB + i, c * P:(c + 1) * P], ident[:, :])
                    last.then_inc(mm_ready, 1)

            def by_token(stage, tb, w, w0):
                for i in range(TPB):
                    ps = bank(stage, tb, i)
                    t0 = (tb * TPB + i) * P
                    for k in range(KC):
                        last = mm(ps[:, 0:DIM], fm[:, k, t0:t0 + P], w[:, k, w0:w0 + DIM],
                                  start=(k == 0), stop=(k == KC - 1))
                    last.then_inc(mm_ready, 1)

            def up(tb):
                for f in range(FF // P):
                    ps = bank("up", tb, f)
                    for k in range(KC):
                        last = mm(ps, w_1[:, k, f * P:(f + 1) * P], fm[:, k, tb * BLK:(tb + 1) * BLK],
                                  start=(k == 0), stop=(k == KC - 1))
                    last.then_inc(mm_ready, 1)

            def down(tb):
                pe.wait_ge(hid_ready, (tb + 1) * (FF // P))
                for i in range(TPB):
                    ps = bank("down", tb, i)
                    for f in range(FF // P):
                        last = mm(ps[:, 0:DIM], hid[tb % 2][:, f, i * P:(i + 1) * P], w_2[:, f, :],
                                  start=(f == 0), stop=(f == FF // P - 1))
                    last.then_inc(mm_ready, 1)

            def dense(stages):
                for stage, tb in stages:
                    if stage == "side":
                        for kind, which in SELF.before[4 * tb:4 * tb + 4]:
                            side("a1", kind, which)
                    elif stage in ("t_a1", "t_a2"):
                        pe.wait_ge(ATT[stage[2:]]["side_read"], SPEC[stage[2:]][0].read("out", last_half(tb)))
                        to_channels(stage, tb)
                    elif stage[:2] == "t_":
                        pe.wait_ge(norm_ready, {"t_ln1": 0, "t_ln2": NT, "t_ln3": 2 * NT}[stage] + (tb + 1) * TPB)
                        to_channels(stage, tb)
                    elif stage == "vals_c":
                        context_values()
                    elif stage in SPLITS:
                        if stage == "proj_q0":
                            pe.wait_ge(in_xT[tb], 16)
                        elif stage in ("proj_q1", "proj_q2"):
                            pe.wait_ge(fm_ready, fm_count("t_ln1" if stage == "proj_q1" else "t_ln2", tb))
                        project(stage, tb)
                    elif stage == "vals_s":
                        by_token(stage, tb, w_sa, 2 * DIM)
                    elif stage in ("out_1", "out_2"):
                        pe.wait_ge(fm_ready, fm_count("t_a1" if stage == "out_1" else "t_a2", tb))
                        by_token(stage, tb, w_so if stage == "out_1" else w_co, 0)
                    elif stage == "up":
                        pe.wait_ge(fm_ready, fm_count("t_ln3", tb))
                        up(tb)
                    else:
                        down(tb)

            def keys_of(att, g, h, kt):
                if att.whole:
                    return Kst[g % att.buffers][:, h, kt * P:(kt + 1) * P]
                b, h0 = g // QUAD, (g % QUAD) * QUAD
                return Kc[:, h0 + h, b * CTX:(b + 1) * CTX]

            def side(name, kind, which):
                att, *_r = SPEC[name]
                s = ATT[name]
                i = att.at[kind, which]
                if i >= att.banks:
                    pe.wait_ge(s["side_read"], i - att.banks + 1)
                ps = side_bank(att, i)
                if kind == "max":
                    q, v = divmod(which, att.units)
                    g, j = divmod(q, HALVES)
                    Q = Qst[g % att.buffers]
                    if v == 0 and j == 0:
                        pe.wait_ge(s["stack_in"][g % att.buffers],
                                   16 * len(BANDS) * (2 if att.whole else 1) * (g // att.buffers + 1))
                    c0 = j * BLK + (v // QUAD if att.whole else v) * P
                    if att.whole:
                        h = v % QUAD
                        for c in range(SEQ // BLK):
                            last = mm(ps[:, c * BLK:(c + 1) * BLK], Q[0:SROWS, h, c0:c0 + P],
                                      Kst[g % att.buffers][0:SROWS, h, c * BLK:(c + 1) * BLK],
                                      start=True, stop=True)
                    else:
                        for h in range(QUAD):
                            last = mm(ps[:, h * CTX:(h + 1) * CTX], Q[0:SROWS, h, c0:c0 + P],
                                      keys_of(att, g, h, 0)[0:SROWS], start=True, stop=True)
                elif kind == "rows":
                    pe.wait_ge(s["mp_ready"], which + 1)
                    for n in range(TPB):
                        last = nc.tensor.transpose(ps.bitcast(BF16)[0:PARTS * QUAD, n * P:(n + 1) * P],
                                                   mp[:, which % 2, n].rearrange("p r h -> p (r h)"), identb[:, :])
                else:
                    pe.wait_ge(s["pv_out"], which + 1)
                    for n in range(TPB):
                        last = nc.tensor.transpose(ps[:, n * P:(n + 1) * P],
                                                   pvT[:, which % 2, n * P:(n + 1) * P], ident[:, :])
                last.then_inc(s["side_done"], 1)

            def attention(name, begin=0):
                att, *_r = SPEC[name]
                s = ATT[name]

                def scores(t, h):
                    q, kt = divmod(t, att.kt)
                    g, j = divmod(q, HALVES)
                    n = t * QUAD + h
                    if kt == 0 and h == 0:
                        pe.wait_ge(s["rows_in"][q % 2], 16 * (q // 2 + 1))
                    if n >= 3:
                        pe.wait_ge(s["exp_done"], n - 2)
                    mm(ST[0:att.keys, n % 3, :], keys_of(att, g, h, kt),
                       Qst[g % att.buffers][:, h, j * BLK:(j + 1) * BLK], start=True, stop=True) \
                        .then_inc(s["st_done"], 1)

                def values(t):
                    q, kt = divmod(t, att.kt)
                    g = q // HALVES
                    if kt == 0:
                        pe.wait_ge(s["vst_ready"], g + 1)
                        if q >= 1:
                            pe.wait_ge(s["pv_out"], q)
                    pe.wait_ge(s["exp_done"], (t + 1) * QUAD)
                    for h in range(QUAD):
                        last = mm(PV[h * 32:(h + 1) * 32, :], Vst[:, g % 2, kt, h, :], prob[:, t % 2, h, :],
                                  start=(kt == 0), stop=(kt == att.kt - 1))
                    last.then_inc(s["pv_done"], 1)

                if not att.whole:
                    pe.wait_ge(s["keys_in"], 16 * len(BANDS))
                for kind, which in att.before[begin:]:
                    side(name, kind, which)
                for t in range(att.steps + 2):
                    work = att.side(t)
                    for h in range(QUAD):
                        if t < att.steps:
                            scores(t, h)
                        for slot, kind, which in work:
                            if slot == h:
                                side(name, kind, which)
                        if h == 1 and 1 <= t <= att.steps:
                            values(t - 1)

            pe.wait_ge(in_ctx, 16 * 6)
            dense(BEFORE_A0)
            pe.wait_ge(pad_ready, 1)
            pe.wait_ge(ident_ready, 1)
            ring_empty("proj_q0", 3)
            attention("a0")
            pe.wait_ge(in_w, 16 * 5)
            pe.wait_ge(pad_ready, 2)
            dense(BEFORE_A1)
            ring_empty("vals_s", 3)
            attention("a1", begin=SELF.ahead * SELF.units)
            dense(BEFORE_A2)
            ring_empty("proj_q2", 3)
            pe.wait_ge(pad_ready, 3)
            attention("a2")
            pe.wait_ge(in_ffn, 32)
            dense(AFTER_A2)

        @block.scalar
        def _(act):
            act_fn = nc.scalar.activation
            with nc.allow_non_contiguous_dma("columns"):
                for c0, src, n in ((C_BQ0, bq0, 2), (C_BK0, bk0, 2), (C_SAQ, sa_b[0:DIM], 2),
                                   (C_SAK, sa_b[DIM:2 * DIM], 2), (C_CQ, cqb, 2), (C_CK, ckb, 2),
                                   (C_G1, g1, 2), (C_B1, b1n, 2), (C_G2, g2, 2), (C_B2, b2n, 2),
                                   (C_G3, g3, 2), (C_B3, b3n, 2), (C_F1, b1, 8)):
                    act.dma_start(cols[:, c0:c0 + n], src.rearrange("(k p) -> p k", p=P)).then_inc(in_b, 16)
                for n, src in ((B_V0, bv0), (B_VS, sa_b[2 * DIM:]), (B_SO, so_b), (B_CV, cvb), (B_CO, cob),
                               (B_F2, b2)):
                    act.dma_start(bc[:, n, :], src.partition_broadcast(P)).then_inc(in_b, 16)
            act.wait_ge(in_b, 16 * 19)
            act.wait_ge(bias_scaled, 1)

            def split_first(stage, tb):
                def second(n, width):
                    act.wait_ge(rest1_ready, n + 1)
                    act_fn(split[:, n % SB, 1, 0:width], r32[:, n % SB, 0:width], ACT.Copy) \
                        .then_inc(part2_ready, 1)
                before = None
                for n, r, mc, _c0, width in chunks(stage, tb):
                    act.wait_ge(mm_ready, r + 1)
                    if n >= SB:
                        act.wait_ge(rest1_ready, n - SB + 1)
                    c = SPLITS[stage][2] + mc
                    act_fn(q32[:, n % SB, 0:width], ring[r % BPR][:, 0:width], ACT.Identity,
                           bias=cols[:, c:c + 1], scale=SPLITS[stage][3]).then_inc(q32_ready, 1)
                    act.wait_ge(q32_ready, n + 1)
                    if n >= SB:
                        act.wait_ge(parts_stored[n % SB], 16 * (n // SB))
                    act_fn(split[:, n % SB, 0, 0:width], q32[:, n % SB, 0:width], ACT.Copy) \
                        .then_inc(part1_ready, 1)
                    if before is not None:
                        second(before, width)
                    before = n
                second(before, width)

            def channels_out(stage, tb, gain=None, bias=None):
                for c in range(KC):
                    r = RING[stage, tb, c]
                    act.wait_ge(mm_ready, r + 1)
                    dst = fm[:, c, tb * BLK:(tb + 1) * BLK]
                    if gain is None:
                        ins = act_fn(dst, ring[r % BPR], ACT.Copy)
                    else:
                        ins = act_fn(dst, ring[r % BPR], ACT.Identity, bias=cols[:, bias + c:bias + c + 1],
                                     scale=cols[:, gain + c:gain + c + 1])
                    ins.then_inc(fm_ready, 1)

            def hidden(tb):
                for f in range(FF // P):
                    r = RING["up", tb, f]
                    act.wait_ge(mm_ready, r + 1)
                    if f == 0 and tb >= 2:
                        act.wait_ge(mm_ready, RING["down", tb - 2, TPB - 1] + 1)
                    act_fn(hid[tb % 2][:, f, :], ring[r % BPR], ACT.Gelu, bias=cols[:, C_F1 + f:C_F1 + f + 1]) \
                        .then_inc(hid_ready, 1)

            def dense(stages):
                for stage, tb in stages:
                    if stage in SPLITS:
                        split_first(stage, tb)
                    elif stage in ("t_a1", "t_a2"):
                        channels_out(stage, tb)
                    elif stage[:2] == "t_":
                        n = int(stage[-1]) - 1
                        channels_out(stage, tb, (C_G1, C_G2, C_G3)[n], (C_B1, C_B2, C_B3)[n])
                    elif stage == "up":
                        hidden(tb)

            def attention(name):
                att, *_r = SPEC[name]
                s = ATT[name]
                for t in range(att.steps + 1):
                    if t < att.steps:
                        if t >= 2:
                            act.wait_ge(s["pv_done"], t - 1)
                        for h in range(QUAD):
                            n = t * QUAD + h
                            act.wait_ge(s["st_done"], n + 1)
                            act_fn(prob[0:att.keys, t % 2, h, :], ST[0:att.keys, n % 3, :], ACT.Exp) \
                                .then_inc(s["exp_done"], 1)
                    if t >= 1 and t % att.kt == 0:
                        q = t // att.kt - 1
                        act.wait_ge(s["pv_done"], t)
                        if q >= 2:
                            act.wait_ge(s["side_done"], att.read("out", q - 2))
                        act_fn(pvT[:, q % 2, :], PV[:, :], ACT.Copy).then_inc(s["pv_out"], 1)

            dense(BEFORE_A0)
            act.wait_ge(pad_ready, 1)
            attention("a0")
            dense(BEFORE_A1)
            attention("a1")
            dense(BEFORE_A2)
            act.wait_ge(pad_ready, 3)
            attention("a2")
            dense(AFTER_A2)

        @block.vector
        def _(dve):
            vec = nc.vector

            def split_rest(stage, tb):
                def third(n, width):
                    dve.wait_ge(part2_ready, n + 1)
                    vec.tensor_tensor(split[:, n % SB, 2, 0:width], r32[:, n % SB, 0:width],
                                      split[:, n % SB, 1, 0:width], ALU.subtract).then_inc(parts_ready, 1)
                before = None
                for n, r, mc, _c0, width in chunks(stage, tb):
                    dve.wait_ge(part1_ready, n + 1)
                    vec.tensor_tensor(r32[:, n % SB, 0:width], q32[:, n % SB, 0:width],
                                      split[:, n % SB, 0, 0:width], ALU.subtract).then_inc(rest1_ready, 1)
                    if before is not None:
                        third(before, width)
                    before = n
                third(before, width)

            def side(name, kind, which):
                att, *_r = SPEC[name]
                s = ATT[name]
                i = att.at[kind, which]
                ps = side_bank(att, i)
                if kind == "max":
                    q, v = divmod(which, att.units)
                    if v == 0 and q >= 2:
                        dve.wait_ge(s["mp_ready"], q - 1)
                    dve.wait_ge(s["side_done"], i + 1)
                    if att.whole:
                        ins = vec.tensor_reduce(nm[:, q % 2, v // QUAD, v % QUAD:v % QUAD + 1], ps, AX.X, ALU.max,
                                                negate=True)
                    else:
                        ins = vec.tensor_reduce(nm[:, q % 2, v, :],
                                                ps[:, 0:QUAD * CTX].rearrange("p (h k) -> p h k", h=QUAD),
                                                AX.X, ALU.max, negate=True)
                elif kind == "rows":
                    if which >= 2:
                        dve.wait_ge(s["rows_in"][which % 2], 16 * (which // 2))
                    dve.wait_ge(s["side_done"], i + 1)
                    ins = vec.tensor_copy(mrow[:, which % 2, :], ps.bitcast(BF16)[0:PARTS * QUAD, 0:BLK])
                else:
                    g, j = divmod(which, HALVES)
                    heads = ps[:, 0:BLK].rearrange("p (i h c) -> p i h c", i=TPB, h=QUAD)
                    dve.wait_ge(s["side_done"], i + 1)
                    vec.reciprocal(rden[:, which % 2], heads[:, :, :, HD:HD + 1].rearrange("p i h c -> p i (h c)")) \
                        .then_inc(s["rd_done"], 1)
                    dve.wait_ge(s["rd_done"], which + 1)
                    b, h0 = g // QUAD, (g % QUAD) * QUAD
                    t0 = b * (SEQ // P) + j * TPB
                    dst = A[:, t0:t0 + TPB, h0 * HD:(h0 + QUAD) * HD].rearrange("p i (h d) -> p i h d", h=QUAD)
                    ins = vec.tensor_tensor(dst, heads[:, :, :, 0:HD],
                                            rden[:, which % 2].unsqueeze(3).to_broadcast([P, TPB, QUAD, HD]),
                                            ALU.mult)
                ins.then_inc(s["side_read"], 1)

            def attention(name, begin=0, extra={}):
                att, *_r = SPEC[name]
                for kind, which in att.before[begin:]:
                    side(name, kind, which)
                for t in range(att.steps + 2):
                    for _slot, kind, which in att.side(t):
                        side(name, kind, which)
                    if t in extra:
                        extra[t]()

            def groups_of(x):
                return x.rearrange("p (g c) -> p g c", g=QUAD)

            def statistics(n, tb):
                for t in range(tb * TPB, (tb + 1) * TPB):
                    dve.wait_ge(x_ready[n], t + 1)
                    vec.bn_stats(stats[:, t, :], X[:, t, :]).then_inc(stat_ready, 1)
                for t in range(tb * TPB, (tb + 1) * TPB):
                    dve.wait_ge(stat_ready, n * NT + t + 1)
                    vec.bn_aggr(mv[:, t, :], stats[:, t, :]).then_inc(mv_ready, 1)

            def normalise(n, tb):
                dve.wait_ge(rstd_ready, n * NB + tb + 1)
                for t in range(tb * TPB, (tb + 1) * TPB):
                    vec.tensor_scalar(A[:, t, :], X[:, t, :], mv[:, t, 0:1], rstd[:, t:t + 1],
                                      ALU.subtract, ALU.mult).then_inc(norm_ready, 1)

            def add_attention(tb):
                dve.wait_ge(ATT["a0"]["side_read"], CROSS.read("out", last_half(tb)))
                for t in range(tb * TPB, (tb + 1) * TPB):
                    vec.tensor_tensor(X[:, t, :], X[:, t, :], A[:, t, :], ALU.add).then_inc(x_ready[0], 1)
                statistics(0, tb)

            def add_product(stage, tb, n):
                dve.wait_ge(bias_added, (n - 1) * NB + tb + 1)
                for i in range(TPB):
                    r = RING[stage, tb, i]
                    dve.wait_ge(mm_ready, r + 1)
                    t = tb * TPB + i
                    vec.tensor_tensor(X[:, t, :], ring[r % BPR][:, 0:DIM], X[:, t, :], ALU.add) \
                        .then_inc(x_ready[n], 1)

            def dense(stages):
                for stage, tb in stages:
                    if stage == "side":
                        for kind, which in SELF.before[4 * tb:4 * tb + 4]:
                            side("a1", kind, which)
                    elif stage == "t_ln1" and tb >= 2:
                        normalise(0, tb)
                    elif stage in ("t_ln2", "t_ln3"):
                        normalise(1 if stage == "t_ln2" else 2, tb)
                    elif stage in SPLITS:
                        split_rest(stage, tb)
                    elif stage in ("out_1", "out_2"):
                        n = 1 if stage == "out_1" else 2
                        add_product(stage, tb, n)
                        statistics(n, tb)
                    elif stage == "down":
                        add_product(stage, tb, 3)
                    elif stage == "vals_s":
                        for i in range(TPB):
                            r, t = RING[stage, tb, i], tb * TPB + i
                            dve.wait_ge(mm_ready, r + 1)
                            vec.tensor_tensor(values_of(t), groups_of(ring[r % BPR][:, 0:DIM]),
                                              groups_of(bc[:, B_VS, :]), ALU.add) \
                                .then_inc(v_ready, 1)
                    elif stage == "vals_c":
                        for a in range(2):
                            for b in range(BATCH):
                                r = RING[stage, 0, a * BATCH + b]
                                dve.wait_ge(mm_ready, r + 1)
                                vec.tensor_tensor(Vc[0:CTX, a, b, :], ring[r % BPR][0:CTX, 0:DIM],
                                                  bc[0:CTX, B_V0 if a == 0 else B_CV, :], ALU.add) \
                                    .then_inc(v_ready, 1)

            dve.wait_ge(in_b, 16 * 19)
            for n, c in enumerate((C_BQ0, C_SAQ, C_CQ)):
                ins = vec.tensor_scalar(cols[:, c:c + 2], cols[:, c:c + 2], SCALE, None, ALU.mult)
            ins.then_inc(bias_scaled, 1)
            dense(BEFORE_A0)
            dve.wait_ge(in_w, 16 * 5)
            vec.tensor_copy(identb[:, :], ident[:, :]).then_inc(ident_ready, 1)
            dve.wait_ge(in_x, 16)
            attention("a0", extra={9: lambda: add_attention(0), 10: lambda: add_attention(1),
                             11: lambda: normalise(0, 0), 12: lambda: normalise(0, 1)})
            add_attention(2)
            add_attention(3)
            dense(BEFORE_A1)
            attention("a1", begin=SELF.ahead * SELF.units)
            dense(BEFORE_A2)
            attention("a2")
            dense(AFTER_A2)

        @block.gpsimd
        def _(pool):
            gp = nc.gpsimd
            def step(ins):
                ins.then_inc(pool_step, 1)
                steps[0] += 1
                pool.wait_ge(pool_step, steps[0])

            steps = [0]
            for n in range(SELF.buffers):
                step(gp.memset(Kst[n][SROWS:P, :, :], 0.0 if n == 1 else 1.0))
                step(gp.memset(Qst[n][SROWS:P, :, :], 0.0))
            step(gp.memset(Vst[:, :, :, :, :], 0.0))
            step(gp.memset(Vst[:, :, :, :, HD:HD + 1], 1.0))
            step(gp.memset(prob[64:P, :, :, :], 0.0))
            step(gp.memset(nexp[:, :], -0.5))
            gp.memset(nr[:, :, :, :], 0.0).then_inc(pad_ready, 1)
            pass

            def stationary(name, g):
                att, _q, _k, vc = SPEC[name]
                s = ATT[name]
                if g >= 2:
                    pool.wait_ge(s["pv_done"], (g - 1) * HALVES * att.kt)
                if att.whole:
                    gp.tensor_copy(Vst[:, g % 2, :, :, 0:HD], V[:, g].rearrange("p k (h d) -> p k h d", h=QUAD)) \
                        .then_inc(s["vst_ready"], 1)
                else:
                    b, h0 = g // QUAD, (g % QUAD) * QUAD
                    src = vc[0:CTX, b, h0 * HD:(h0 + QUAD) * HD]
                    gp.tensor_copy(Vst[0:CTX, g % 2, 0, :, 0:HD], src.rearrange("p (h d) -> p h d", h=QUAD)) \
                        .then_inc(s["vst_ready"], 1)

            def parts_of_maxima(name, q):
                att, *_r = SPEC[name]
                s = ATT[name]
                pool.wait_ge(s["side_read"], att.read("max", (q + 1) * att.units - 1))
                if q >= 2:
                    pool.wait_ge(s["side_done"], att.read("rows", q - 2))
                a, r, m = nm[:, q % 2], nr[:, q % 2], mp[:, q % 2]
                gp.tensor_copy(m[:, :, 0, :], a).then_inc(s["mp_p1"], 1)
                pool.wait_ge(s["mp_p1"], q + 1)
                gp.tensor_tensor(r, a, m[:, :, 0, :], ALU.subtract).then_inc(s["mp_r1"], 1)
                pool.wait_ge(s["mp_r1"], q + 1)
                gp.tensor_copy(m[:, :, 1, :], r).then_inc(s["mp_p2"], 1)
                pool.wait_ge(s["mp_p2"], q + 1)
                gp.tensor_tensor(m[:, :, 2, :], r, m[:, :, 1, :], ALU.subtract).then_inc(s["mp_ready"], 1)

            def attention(name, extra={}):
                att, *_r = SPEC[name]
                for q in range(NQ - att.ahead):
                    if q % 2 == 0 and q // 2 + 1 < NG:
                        stationary(name, q // 2 + 1)
                    parts_of_maxima(name, q + att.ahead)
                    if q in extra:
                        extra[q]()
                for g in range((NQ - att.ahead + 1) // 2 + 1, NG):
                    stationary(name, g)

            def rsqrt(n, tb):
                pool.wait_ge(mv_ready, n * NT + (tb + 1) * TPB)
                a = rstd[:, tb * TPB:(tb + 1) * TPB]
                gp.tensor_scalar(a, mv[:, tb * TPB:(tb + 1) * TPB, 1], EPS, None, ALU.add).then_inc(var_ready, 1)
                pool.wait_ge(var_ready, n * NB + tb + 1)
                gp.tensor_tensor(a, a, nexp[:, 0:TPB], ALU.pow).then_inc(rstd_ready, 1)

            def add_bias(n, which, tb):
                pool.wait_ge(norm_ready, n * NT + (tb + 1) * TPB)
                for t in range(tb * TPB, (tb + 1) * TPB):
                    ins = gp.tensor_tensor(X[:, t, :], X[:, t, :], bc[:, which, :], ALU.add)
                ins.then_inc(bias_added, 1)

            pool.wait_ge(v_ready, 4)
            stationary("a0", 0)
            for q in range(CROSS.ahead):
                parts_of_maxima("a0", q)
            attention("a0", {10: lambda: rsqrt(0, 0), 11: lambda: rsqrt(0, 1)})
            pool.wait_ge(ATT["a0"]["st_done"], CROSS.steps * QUAD)
            pool.wait_ge(ATT["a0"]["vst_ready"], NG)
            step(gp.memset(Kst[1][SROWS:P, :, :], 1.0))
            gp.memset(nr[:, :, :, :], 0.0).then_inc(pad_ready, 1)
            rsqrt(0, 2)
            rsqrt(0, 3)
            pool.wait_ge(v_ready, 4 + NT // BATCH)
            stationary("a1", 0)
            for tb in range(NB):
                add_bias(0, B_SO, tb)
            for q in range(SELF.ahead):
                parts_of_maxima("a1", q)
            pool.wait_ge(v_ready, 4 + NT)
            attention("a1")
            for tb in range(NB):
                rsqrt(1, tb)
                if tb >= 1:
                    add_bias(1, B_CO, tb - 1)
            pool.wait_ge(ATT["a1"]["pv_done"], SELF.steps)
            pool.wait_ge(bias_added, 2 * NB - 1)
            step(gp.memset(prob[64:P, :, :, :], 0.0))
            step(gp.memset(Kst[1][SROWS:P, :, :], 0.0))
            step(gp.memset(Vst[64:P, :, 0, :, :], 0.0))
            step(gp.memset(Vst[0:CTX, :, 0, :, HD:HD + 1], 1.0))
            gp.memset(nr[:, :, :, :], 0.0).then_inc(pad_ready, 1)
            add_bias(1, B_CO, NB - 1)
            stationary("a2", 0)
            for q in range(CROSS.ahead):
                parts_of_maxima("a2", q)
            attention("a2")
            rsqrt(2, 0)
            rsqrt(2, 1)
            add_bias(2, B_F2, 0)
            rsqrt(2, 2)
            add_bias(2, B_F2, 1)
            rsqrt(2, 3)
            add_bias(2, B_F2, 2)
            add_bias(2, B_F2, 3)


def kernel(**inputs):
    import numpy as _np
    import concourse.bacc as _bacc
    from concourse import mybir as _mybir
    from concourse.bass_utils import run_bass_kernel_spmd as _run

    g = {k: _np.asarray(v) for k, v in inputs.items()}
    x = g["x"].reshape(TOK, DIM)
    c = g["ctx_1024"].reshape(BATCH * CTX, DIM)
    L0 = {k[9:]: v for k, v in g.items() if k.startswith("L0_xattn_")}
    L1 = {k[9:]: v for k, v in g.items() if k.startswith("L1_xattn_")}
    arrays = [
        ("xT", x.T), ("x", x), ("ctxT", c.T), ("ident", _np.eye(P, dtype=_np.float32)),
        ("wq0", L0["Wq"]), ("bq0", L0["bq"]), ("wk0", L0["Wk"]), ("bk0", L0["bk"]),
        ("wv0", L0["Wv"]), ("bv0", L0["bv"]),
        ("sa_w", L1["sa_in_w"].T), ("sa_b", L1["sa_in_b"]), ("so_w", L1["sa_out_w"].T), ("so_b", L1["sa_out_b"]),
        ("g1", L1["ln1_g"]), ("b1n", L1["ln1_b"]), ("cqw", L1["cq_w"].T), ("cqb", L1["cq_b"]),
        ("ckw", L1["ck_w"].T), ("ckb", L1["ck_b"]), ("cvw", L1["cv_w"].T), ("cvb", L1["cv_b"]),
        ("cow", L1["co_w"].T), ("cob", L1["co_b"]), ("g2", L1["ln2_g"]), ("b2n", L1["ln2_b"]),
        ("w1", L1["w1"].T), ("b1", L1["b1"]), ("w2", L1["w2"].T), ("b2", L1["b2"]),
        ("g3", L1["ln3_g"]), ("b3n", L1["ln3_b"]),
    ]
    nc = _bacc.Bacc("TRN2", target_bir_lowering=False, num_devices=1)
    feeds, args = {}, []
    for name, a in arrays:
        a = _np.ascontiguousarray(a)
        feeds[f"in_{name}"] = a
        args.append(nc.dram_tensor(f"in_{name}", a.shape, _mybir.dt.from_np(a.dtype), kind="ExternalInput").ap())
    args.append(nc.dram_tensor("out_0", (TOK, DIM), _mybir.dt.float32, kind="ExternalOutput").ap())
    xattn_kernel(nc, *args)
    r = _run(nc, [feeds], core_ids=[0])
    return r.results[0]["out_0"].reshape(BATCH, SEQ, DIM)
```
